# Optimizing a Trainium2 kernel written in Bass

```python
import numpy as np
import jax
import jax.numpy as jnp

def _softmax(x, axis=-1):
    return jax.nn.softmax(x, axis=axis)

def _gelu(x):
    return jax.nn.gelu(x, approximate=True)

def _silu(x):
    return jax.nn.silu(x)

def _sigmoid(x):
    return jax.nn.sigmoid(x)

def _layernorm(x, axis=-1, eps=1e-05):
    m = jnp.mean(x, axis=axis, keepdims=True)
    v = jnp.var(x, axis=axis, keepdims=True)
    return (x - m) / jnp.sqrt(v + eps)

def _scatter_add(tgt, idx, src, axis=0):
    return tgt.at[idx].add(src)

def _segment_sum(src, seg, n):
    return jax.ops.segment_sum(src, seg, n)
kernel_name = 'mk_xattn_seq_d2_seqx_r2_f949a3'

def setup_inputs(seed: int=0):
    np.random.seed(seed)
    _w = jnp.asarray

    def _rec_inputs():
        import jax
        import jax.numpy as jnp
        _rk = jax.random.key(seed)
        x = -0.0001108 + 0.9999 * jax.random.normal(jax.random.fold_in(_rk, 1), (8, 100, 640), jnp.float32)
        _lenS = 100 - jax.random.randint(jax.random.fold_in(_rk, 7), (8,), 0, max(1, 100 // 4) + 1, jnp.int32)
        _lenS2 = 722 - jax.random.randint(jax.random.fold_in(_rk, 8), (8,), 0, max(1, 722 // 4) + 1, jnp.int32)
        _ctx_2048P = jax.random.normal(jax.random.fold_in(_rk, 11), (8, 16, 1024), jnp.float32)
        _ctx_2048c = jax.random.dirichlet(jax.random.fold_in(_rk, 511), 0.3 * jnp.ones((16,), jnp.float32), (8, 722))
        _ctx_2048t = jnp.einsum('bsk,bkd->bsd', _ctx_2048c, _ctx_2048P)
        _ctx_2048t = _ctx_2048t * jax.lax.rsqrt(jnp.mean(jnp.square(_ctx_2048t)) + 1e-12) * 0.953939
        ctx_2048 = -0.000395056 + 1.00006 * (_ctx_2048t + 0.3 * jax.random.normal(jax.random.fold_in(_rk, 611), (8, 722, 1024), jnp.float32))
        fside_S_0 = jax.random.uniform(jax.random.fold_in(_rk, 12), (100,), jnp.float32, 0.0, 0.999707)
        return (x, ctx_2048, fside_S_0)
    x, ctx_2048, fside_S_0 = _rec_inputs()

    def _L0_xattn_setup():
        import jax, jax.numpy as jnp
        import numpy as np
        NUM_HEADS = 20
        TEXT_LEN = 77
        IP_SCALE = 1.0

        def _attend(q, k, v, sm_scale):
            scores = jnp.einsum('bhsd,bhld->bhsl', q, k) * sm_scale
            probs = jax.nn.softmax(scores, axis=-1)
            return jnp.einsum('bhsl,bhld->bhsd', probs, v)

        def _split_heads(x, h):
            b, s, c = x.shape
            return x.reshape(b, s, h, c // h).transpose(0, 2, 1, 3)

        def _merge_heads(x):
            b, h, s, d = x.shape
            return x.transpose(0, 2, 1, 3).reshape(b, s, h * d)
        key = jax.random.key(seed)
        ks = jax.random.split(key, 8)
        B, S, C, CC, L = (8, 2048, 640, 1024, TEXT_LEN + 4)
        sd_q = 1.0 / np.sqrt(C)
        sd_kv = 1.0 / np.sqrt(CC)
        return {'hidden_states': jax.random.normal(ks[0], (B, S, C), jnp.float32), 'encoder_hidden_states': jax.random.normal(ks[1], (B, L, CC), jnp.float32), 'Wq': jax.random.normal(ks[2], (C, C), jnp.float32) * sd_q, 'Wk': jax.random.normal(ks[3], (C, CC), jnp.float32) * sd_kv, 'Wv': jax.random.normal(ks[4], (C, CC), jnp.float32) * sd_kv, 'Wk_ip': jax.random.normal(ks[5], (C, CC), jnp.float32) * sd_kv, 'Wv_ip': jax.random.normal(ks[6], (C, CC), jnp.float32) * sd_kv, 'Wo': jax.random.normal(ks[7], (C, C), jnp.float32) * sd_q, 'bo': jnp.zeros((C,), jnp.float32)}
    _L0_xattn_all = _L0_xattn_setup()
    _L0_xattn_in = {k: v for k, v in _L0_xattn_all.items() if k in ('Wq', 'Wk', 'Wv', 'Wk_ip', 'Wv_ip', 'Wo', 'bo')}
    del _L0_xattn_all

    def _L1_xattn_setup():
        import jax, jax.numpy as jnp
        import numpy as np
        import math
        HEADS = 20
        NUM_TOKENS = 4
        SEM_SCALE = 0.5
        IP_SCALE = 1.0
        TEXT_LEN = 77

        def _split_heads(x, B, H, D):
            return x.reshape(B, -1, H, D).transpose(0, 2, 1, 3)
        key = jax.random.key(seed)
        ks = jax.random.split(key, 10)
        B, S, C, CD = (4, 2048, 640, 1024)

        def g(k, shape, std=1.0):
            return jax.random.normal(k, shape, dtype=jnp.float32) * std
        return {'hidden_states': g(ks[0], (B, S, C)), 'encoder_hidden_states': g(ks[1], (B, TEXT_LEN + NUM_TOKENS, CD)), 'spatial_mask': jax.random.uniform(ks[2], (S,), dtype=jnp.float32), 'Wq': g(ks[3], (C, C), 1.0 / math.sqrt(C)), 'Wk': g(ks[4], (CD, C), 1.0 / math.sqrt(CD)), 'Wv': g(ks[5], (CD, C), 1.0 / math.sqrt(CD)), 'Wk_ip': g(ks[6], (CD, C), 1.0 / math.sqrt(CD)), 'Wv_ip': g(ks[7], (CD, C), 1.0 / math.sqrt(CD)), 'Wout': g(ks[8], (C, C), 1.0 / math.sqrt(C)), 'bout': jnp.zeros((C,), dtype=jnp.float32)}
    _L1_xattn_all = _L1_xattn_setup()
    _L1_xattn_in = {k: v for k, v in _L1_xattn_all.items() if k in ('Wq', 'Wk', 'Wv', 'Wk_ip', 'Wv_ip', 'Wout', 'bout')}
    del _L1_xattn_all
    return {'x': x, 'ctx_2048': ctx_2048, 'fside_S_0': fside_S_0, 'L0_xattn_Wq': _L0_xattn_in['Wq'], 'L0_xattn_Wk': _L0_xattn_in['Wk'], 'L0_xattn_Wv': _L0_xattn_in['Wv'], 'L0_xattn_Wk_ip': _L0_xattn_in['Wk_ip'], 'L0_xattn_Wv_ip': _L0_xattn_in['Wv_ip'], 'L0_xattn_Wo': _L0_xattn_in['Wo'], 'L0_xattn_bo': _L0_xattn_in['bo'], 'L1_xattn_Wq': _L1_xattn_in['Wq'], 'L1_xattn_Wk': _L1_xattn_in['Wk'], 'L1_xattn_Wv': _L1_xattn_in['Wv'], 'L1_xattn_Wk_ip': _L1_xattn_in['Wk_ip'], 'L1_xattn_Wv_ip': _L1_xattn_in['Wv_ip'], 'L1_xattn_Wout': _L1_xattn_in['Wout'], 'L1_xattn_bout': _L1_xattn_in['bout']}

def reference(x, ctx_2048, fside_S_0, L0_xattn_Wq, L0_xattn_Wk, L0_xattn_Wv, L0_xattn_Wk_ip, L0_xattn_Wv_ip, L0_xattn_Wo, L0_xattn_bo, L1_xattn_Wq, L1_xattn_Wk, L1_xattn_Wv, L1_xattn_Wk_ip, L1_xattn_Wv_ip, L1_xattn_Wout, L1_xattn_bout):
    import jax
    import jax.numpy as jnp

    def _L0_xattn_ref(hidden_states, encoder_hidden_states, Wq, Wk, Wv, Wk_ip, Wv_ip, Wo, bo):
        import jax, jax.numpy as jnp
        import numpy as np
        NUM_HEADS = 20
        TEXT_LEN = 77
        IP_SCALE = 1.0

        def _attend(q, k, v, sm_scale):
            scores = jnp.einsum('bhsd,bhld->bhsl', q, k) * sm_scale
            probs = jax.nn.softmax(scores, axis=-1)
            return jnp.einsum('bhsl,bhld->bhsd', probs, v)

        def _split_heads(x, h):
            b, s, c = x.shape
            return x.reshape(b, s, h, c // h).transpose(0, 2, 1, 3)

        def _merge_heads(x):
            b, h, s, d = x.shape
            return x.transpose(0, 2, 1, 3).reshape(b, s, h * d)
        residual = hidden_states
        B, S, C = hidden_states.shape
        H = NUM_HEADS
        D = C // H
        sm_scale = 1.0 / jnp.sqrt(jnp.asarray(D, hidden_states.dtype))
        text = encoder_hidden_states[:, :TEXT_LEN, :]
        ip = encoder_hidden_states[:, TEXT_LEN:, :]
        q = _split_heads(hidden_states @ Wq.T, H)
        k = _split_heads(text @ Wk.T, H)
        v = _split_heads(text @ Wv.T, H)
        out_text = _merge_heads(_attend(q, k, v, sm_scale))
        k_ip = _split_heads(ip @ Wk_ip.T, H)
        v_ip = _split_heads(ip @ Wv_ip.T, H)
        out_ip = _merge_heads(_attend(q, k_ip, v_ip, sm_scale))
        out = out_text + IP_SCALE * out_ip
        out = out @ Wo.T + bo
        return out + residual

    def _L1_xattn_ref(hidden_states, encoder_hidden_states, spatial_mask, Wq, Wk, Wv, Wk_ip, Wv_ip, Wout, bout):
        import jax, jax.numpy as jnp
        import numpy as np
        import math
        HEADS = 20
        NUM_TOKENS = 4
        SEM_SCALE = 0.5
        IP_SCALE = 1.0
        TEXT_LEN = 77

        def _split_heads(x, B, H, D):
            return x.reshape(B, -1, H, D).transpose(0, 2, 1, 3)
        B, S, C = hidden_states.shape
        D = C // HEADS
        scale = 1.0 / math.sqrt(D)
        residual = hidden_states
        text = encoder_hidden_states[:, :TEXT_LEN]
        ip = encoder_hidden_states[:, TEXT_LEN:]
        q = hidden_states @ Wq
        k_text = text @ Wk
        v_text = text @ Wv
        q_h = _split_heads(q, B, HEADS, D)
        k_h = _split_heads(k_text, B, HEADS, D)
        v_h = _split_heads(v_text, B, HEADS, D)
        logits = jnp.einsum('bhqd,bhkd->bhqk', q_h, k_h) * scale
        probs = jax.nn.softmax(logits, axis=-1)
        text_out = jnp.einsum('bhqk,bhkd->bhqd', probs, v_h)
        text_out = text_out.transpose(0, 2, 1, 3).reshape(B, S, C)
        ip_k = ip @ Wk_ip
        ip_v = ip @ Wv_ip
        ip_k_h = _split_heads(ip_k, B, HEADS, D)
        ip_v_h = _split_heads(ip_v, B, HEADS, D)
        scores = jnp.einsum('bhqd,bhkd->bhqk', q_h, ip_k_h) * scale
        text_probs = jax.nn.softmax(jnp.einsum('bqc,bkc->bqk', q, k_text) * scale, axis=-1)
        q_sem = jnp.einsum('bqk,bkc->bqc', text_probs, text)
        sem = jnp.einsum('bqc,bnc->bqn', q_sem, ip) * scale
        sem = jax.lax.stop_gradient(sem)
        fused = scores + SEM_SCALE * sem[:, None, :, :]
        ip_probs = jax.nn.softmax(fused, axis=-1)
        ip_probs = ip_probs * spatial_mask[None, None, :, None]
        ip_out = jnp.einsum('bhqk,bhkd->bhqd', ip_probs, ip_v_h)
        ip_out = ip_out.transpose(0, 2, 1, 3).reshape(B, S, C)
        hs = text_out + IP_SCALE * ip_out
        out = hs @ Wout + bout
        out = out + residual
        return out
    x = _L0_xattn_ref(x, ctx_2048, L0_xattn_Wq, L0_xattn_Wk, L0_xattn_Wv, L0_xattn_Wk_ip, L0_xattn_Wv_ip, L0_xattn_Wo, L0_xattn_bo)
    x = _L1_xattn_ref(x, ctx_2048, fside_S_0, L1_xattn_Wq, L1_xattn_Wk, L1_xattn_Wv, L1_xattn_Wk_ip, L1_xattn_Wv_ip, L1_xattn_Wout, L1_xattn_bout)
    return x

_drawn_inputs = setup_inputs


def setup_inputs(seed=0):
    import zlib

    import numpy as np

    out = dict(_drawn_inputs(seed))
    spreads = {'L0_xattn_bo': (0.0, 0.1), 'L1_xattn_bout': (0.0, 0.1)}
    factors = {}
    for name, (base, spread) in spreads.items():
        noise = np.random.default_rng([zlib.crc32(name.encode()), seed]).standard_normal(out[name].shape)
        drawn = base * np.exp(spread * noise) if base else spread * noise
        out[name] = jnp.asarray(drawn.astype(out[name].dtype))
    for name, factor in factors.items():
        out[name] = (out[name] * factor).astype(out[name].dtype)
    return out
```

```python
from contextlib import ExitStack

import concourse.bass as bass
import numpy as np
from concourse import mybir

ALU = mybir.AluOpType
ACT = mybir.ActivationFunctionType
AX = mybir.AxisListType
F32 = mybir.dt.float32
F32R = mybir.dt.float32r
F16 = mybir.dt.float16
BF16 = mybir.dt.bfloat16
I32 = mybir.dt.int32
RMAX = bass.bass_isa.ReduceOp.max

P = 128
B, S, C, CC = 8, 100, 640, 1024
TOK = 722
H, D = 20, 32
TEXT = 77
IP = TOK - TEXT
LAYERS = 2
HG = P // D
G = H // HG
KT = CC // P
CT = C // P
KEY = 108
NIP = -(-IP // KEY)
NT = 1 + NIP
TP = TEXT + 1
IPP = KEY * NIP
HALF = IPP // 2
LAST = IP - KEY * (NIP - 1)
TOKP = TP + IPP
Q4 = HG * S
VS = 3 * D + 2
PW = Q4 + 32
MT = B * S // 2
STEPS = B * G
SC = float(D) ** -0.5
SEM = 0.5
TINY = 1e-30
TOP = 2.0 ** 14
EXP_BITS = 0x7F800000
LOWEST = -3.0e38


def xattn_pair_kernel(nc, ctx_d, x_d, w_d, wq_d, wo_d, bias_d, mask_d, const_d, x1_d, out_d):
    with ExitStack() as stack:
        def sb(name, shape, dt):
            return stack.enter_context(nc.sbuf_tensor(name, shape, dt))

        def psum(name, shape, dt=F32):
            return stack.enter_context(nc.psum_tensor(name, shape, dt))

        def sem(name):
            return stack.enter_context(nc.semaphore(name))

        w_hi = sb("w_hi", [P, 4, KT, C], F16)
        w_lo = sb("w_lo", [P, 4, KT, C], F16)
        c_hi = sb("c_hi", [P, KT, TOKP], F16)
        c_lo = sb("c_lo", [P, KT, TOKP], F16)
        raw = sb("raw", [P, KT * TOKP], F32)
        ctx_raw = raw[:, :].rearrange("p (k t) -> p k t", k=KT)
        xh = raw[:, 0:CT * MT].rearrange("p (c t) -> p c t", c=CT)
        wq = raw[:, CT * MT:CT * MT + CT * C].rearrange("p (k n) -> p k n", k=CT)
        qo = sb("qo", [P, CT, B * S], F32)
        work = sb("work", [P, 2744 + TOKP + 512 + 3 * Q4], F32)
        w_raw = work[:, 0:KT * C]
        vst = work[:, 0:2744].bitcast(BF16).rearrange("p (b t h v) -> p b t h v", b=2, t=NT, h=HG)
        vT = work[:, 2744:2744 + TOKP]
        v_rest = work[:, 2744 + TOKP:2744 + TOKP + 512]
        prob = work[:, 2744 + TOKP + 512:2744 + TOKP + 512 + 3 * Q4].rearrange("p (r q) -> p r q", r=3)
        pwork = sb("pwork", [P, CT * C], F32)
        wo = pwork[:, :].rearrange("p (k n) -> p k n", k=CT)
        sel_raw = pwork[:, 0:2 * KEY]
        p_hi = pwork[:, 0:NT * PW // 2].bitcast(F16).rearrange("p (t q) -> p t q", t=NT)
        p_lo = pwork[:, NT * PW // 2:NT * PW].bitcast(F16).rearrange("p (t q) -> p t q", t=NT)
        k_hi = sb("k_hi", [P, 2, IPP], F32R)
        k_lo = sb("k_lo", [P, 2, IPP], F32R)
        kt32 = sb("kt32", [P, G, TP], F32)
        kt_hi = sb("kt_hi", [P, G, TP], F32R)
        kt_lo = sb("kt_lo", [P, G, TP], F32R)
        q_row = sb("q_row", [P, CT, S], F32)
        qbd = sb("qbd", [P, HG, S], F32)
        q_hi = sb("q_hi", [P, HG, S], F32R)
        q_lo = sb("q_lo", [P, HG, S], F32R)
        shift = sb("shift", [P, HG, S], F32R)
        sel = sb("sel", [P, 2, KEY], F32R)
        const = sb("const", [P, P + 3 * HG], F32)
        ident = const[:, 0:P]
        hmask = const[:, P:P + HG]
        nmask = const[:, P + HG:P + 2 * HG]
        ones = const[:, P + 2 * HG:P + 3 * HG]
        bias = sb("bias", [P, LAYERS, CT], F32)
        mask = sb("mask", [S, LAYERS], F32)
        mx = sb("mx", [S, P], F32)
        semq = sb("semq", [S, 2, HALF], F32)
        semk = sb("semk", [KEY, NIP, S], F32)
        ti = sb("ti", [P, 2, HALF], F32)
        pT = sb("pT", [TEXT, S], F32)
        acc = sb("acc", [S, 2, HG, D], F32)
        den = sb("den", [S, 2, HG], F32)
        wscale = sb("wscale", [P, 4], F32)
        winv = sb("winv", [P, 4], F32)
        cs = sb("cs", [P, 8], F32)
        ws = sb("ws", [P, 4], F32)
        inv = sb("inv", [P, 4], F32)
        sm = sb("sm", [S, 4], F32)
        primer = sb("primer", [1, 16], F32)

        bankA, bankB = psum("bankA", [P, 512]), psum("bankB", [P, 512])
        rows = psum("rows", [P, 2, 512])
        st = psum("st", [P, 2, 512])
        pv = psum("pv", [P, 2, 512])
        banks = (bankA, bankB)

        const_in, sel_ok = sem("const_in"), sem("sel_ok")
        w_in, w_chain, w_high, w_low = sem("w_in"), sem("w_chain"), sem("w_high"), sem("w_low")
        ctx_in, ctx_chain, ctx_high, ctx_low = sem("ctx_in"), sem("ctx_chain"), sem("ctx_high"), sem("ctx_low")
        wq_in, wo_in, xh_in = sem("wq_in"), sem("wo_in"), sem("xh_in")
        x1_out, y_out = sem("x1_out"), sem("y_out")
        lin_full, q_evac, out_evac = sem("lin_full"), sem("q_evac"), sem("out_evac")
        row_full, row_free = sem("row_full"), sem("row_free")
        kt_high, kt_low = sem("kt_high"), sem("kt_low")
        k_full, k_high, k_low = sem("k_full"), sem("k_high"), sem("k_low")
        v_full, vT_ok, vt_full = sem("v_full"), sem("vT_ok"), sem("vt_full")
        v_high, v_res, v_mid, v_parts = sem("v_high"), sem("v_res"), sem("v_mid"), sem("v_parts")
        qrow_ok, qbd_ok, q_high, q_low = sem("qrow_ok"), sem("qbd_ok"), sem("q_high"), sem("q_low")
        s_full, sadd, p_high, p_low = sem("s_full"), sem("sadd"), sem("p_high"), sem("p_low")
        pv_full, pv_read, norm, o_sum = sem("pv_full"), sem("pv_read"), sem("norm"), sem("o_sum")
        probs, pads, inv_ok = sem("probs"), sem("pads"), sem("inv_ok")

        PRIMED = (s_full, pv_full, p_high, p_low, row_free, vt_full, v_res, v_parts, q_low, pv_read, qrow_ok)

        def after(eng, s, n):
            eng.wait_ge(s, n + 1 if s in PRIMED else n)

        def row_uses(l):
            names = [("kt", 0)] + ([(n, 0) for n in ("logit", "pT", "ti", "semq", "semk")] if l else [])
            for g in range(G):
                names.append(("max0", g))
                if g:
                    names.append(("oT", g - 1))
                names += [("max1", g), ("max2", g), ("max3", g), ("shift", g)]
                if g == G - 1:
                    names.append(("cmax", g))
            return names + [("oT", G - 1)]

        ROWS = [row_uses(l) for l in range(LAYERS)]

        def row_use(l, i, name, g=0):
            return i * len(ROWS[l]) + (l * B * len(ROWS[0]) + ROWS[l].index((name, g)))

        def step(l, i, g):
            return i * G + (l * STEPS + g)

        block = stack.enter_context(nc.Block())

        @block.sync
        def _(sp):
            sp.dma_start(const[:], const_d[:, 0:P + 3 * HG]).then_inc(const_in, 16)
            sp.dma_start(sel_raw, const_d[:, P + 3 * HG:]).then_inc(const_in, 16)
            sp.dma_start(bias[:], bias_d).then_inc(const_in, 16)
            sp.dma_start(mask[:], mask_d).then_inc(const_in, 16)
            sp.dma_start(raw[:], ctx_d[0]).then_inc(ctx_in, 16)

            def linear_half(l, half, first):
                sp.dma_start(xh, (x1_d if l == LAYERS else x_d)[half]).then_inc(xh_in, 16)

            for l in range(LAYERS):
                sp.wait_ge(ctx_low, KT * (l * B + 1))
                sp.dma_start(wq, wq_d[l]).then_inc(wq_in, 16)
                for half in range(2):
                    if half:
                        sp.wait_ge(q_evac, CT * (2 * l + 1))
                        if l:
                            sp.wait_ge(x1_out, 16)
                    sp.dma_start(xh, x_d[half]).then_inc(xh_in, 16)
                    if l == 1:
                        if half == 0:
                            after(sp, pv_full, STEPS)
                            sp.dma_start(wo, wo_d[0]).then_inc(wo_in, 16)
                        sp.wait_ge(out_evac, CT * (half + 1))
                        sp.dma_start(x1_d[half], xh).then_inc(x1_out, 16)
                sp.wait_ge(q_evac, CT * 2 * (l + 1))
                if l:
                    sp.wait_ge(x1_out, 32)
                with sp.Fori(0, B) as i:
                    sp.wait_ge(ctx_low, i * KT + KT * (l * B + 1))
                    sp.dma_start(raw[:], ctx_d[bass.ds(i + 1, 1)].rearrange("o p n -> (o p) n")).then_inc(ctx_in, 16)
            sp.wait_ge(ctx_low, KT * (LAYERS * B + 1))
            sp.dma_start(xh, x1_d[0]).then_inc(xh_in, 16)
            after(sp, pv_full, LAYERS * STEPS)
            sp.dma_start(wo, wo_d[1]).then_inc(wo_in, 16)
            for half in range(2):
                if half:
                    sp.wait_ge(y_out, 16)
                    sp.dma_start(xh, x1_d[1]).then_inc(xh_in, 16)
                sp.wait_ge(out_evac, CT * (half + 3))
                sp.dma_start(out_d[half], xh).then_inc(y_out, 16)
            sp.wait_ge(y_out, 32)

        @block.tensor
        def _(pe):
            lin = [0]

            def linear(weight, src, half, evac_of):
                for c in range(CT):
                    n = lin[0]
                    if c >= 2:
                        pe.wait_ge(evac_of, CT * half + c - 1)
                    for k in range(CT):
                        mm = nc.tensor.matmul(banks[n % 2][:, 0:MT], weight[:, k, c * P:(c + 1) * P], src(k),
                                              start=(k == 0), stop=(k == CT - 1))
                    mm.then_inc(lin_full, 1)
                    lin[0] += 1

            def out_phase(l):
                for half in range(2):
                    pe.wait_ge(wo_in, 16 * (l + 1))
                    pe.wait_ge(q_evac, CT * (2 * (l + 1) + (half if l == 0 else 0)))
                    if half and l == 1:
                        pe.wait_ge(out_evac, CT * 3)
                    linear(wo, lambda k: qo[:, k, half * MT:(half + 1) * MT], 2 * l + half, out_evac)
                    if l == 0:
                        q_half(1, half)

            def q_half(l, half):
                pe.wait_ge(wq_in, 16 * (l + 1))
                if l:
                    pe.wait_ge(out_evac, CT * (half + 1))
                else:
                    pe.wait_ge(xh_in, 16 * (half + 1))
                    if half:
                        pe.wait_ge(q_evac, CT)
                linear(wq, lambda k: xh[:, k, :], 2 * l + half, q_evac)

            def pairs(out, hi_lo_w, hi_lo_x, n_k, each_k=None):
                for k in range(n_k):
                    if each_k:
                        each_k(k)
                    for m, (a, b) in enumerate(((0, 0), (0, 1), (1, 0))):
                        mm = nc.tensor.matmul(out, hi_lo_w[a](k), hi_lo_x[b](k), start=(k == 0 and m == 0),
                                              stop=(k == n_k - 1 and m == 2))
                return mm

            def weights(w, g):
                return [lambda k, t=t: t[:, w, k, g * P:(g + 1) * P] for t in (w_hi, w_lo)]

            def tokens(a, b):
                return [lambda k, t=t: t[:, k, a:b] for t in (c_hi, c_lo)]

            def k_text(l, i):
                after(pe, row_free, row_use(l, i, "kt"))
                for g in range(G):
                    each = (lambda k: pe.wait_ge(ctx_low, i * KT + (KT * l * B + k + 1))) if g == 0 else None
                    mm = pairs(rows[:, 0, g * TP:(g + 1) * TP], weights(0, g), tokens(0, TP), KT, each)
                mm.then_inc(row_full, 1)

            def k_unit(l, i, g, c):
                u = step(l, i, g)
                after(pe, v_res, 2 * u)
                pairs(banks[c][:, 0:HALF], weights(1, g), tokens(TP + c * HALF, TP + (c + 1) * HALF),
                      KT).then_inc(k_full, 1)

            def v_unit(l, i, g, c):
                u = step(l, i, g)
                pe.wait_ge(k_low, 2 * u + (c + 1))
                if c == 0:
                    pairs(bankA[:, 0:TP], weights(2, g), tokens(0, TP), KT)
                    mm = pairs(bankA[:, TP:TP + HALF], weights(3, g), tokens(TP, TP + HALF), KT)
                else:
                    mm = pairs(bankB[:, 0:HALF], weights(3, g), tokens(TP + HALF, TOKP), KT)
                mm.then_inc(v_full, 1)

            def v_turn(l, i, g, c):
                u = step(l, i, g)
                pe.wait_ge(vT_ok, 2 * u + (c + 1))
                for n, t in enumerate(range(4) if c == 0 else range(4, NT)):
                    a = TP + (t - 1) * KEY if t else 0
                    mm = nc.tensor.transpose(banks[c][0:KEY, n * P:(n + 1) * P], vT[:, a:a + KEY], ident)
                mm.then_inc(vt_full, 1)

            def max_scores(l, i, g, h):
                t = step(l, i, g)
                if h == 0:
                    pe.wait_ge(q_high, t + 1)
                    pe.wait_ge(k_high, 2 * t + 2)
                    pe.wait_ge(kt_high, i + (l * B + 1))
                after(pe, row_free, row_use(l, i, f"max{h}", g))
                nc.tensor.matmul(rows[0:S, 0, 0:HALF], q_hi[:, h, :], k_hi[:, g % 2, 0:HALF], start=True, stop=True)
                nc.tensor.matmul(rows[0:S, 0, HALF:HALF + TP], q_hi[:, h, :], kt_hi[:, g, :], start=True, stop=True)
                nc.tensor.matmul(rows[0:S, 1, 0:HALF], q_hi[:, h, :], k_hi[:, g % 2, HALF:IPP],
                                 start=True, stop=True).then_inc(row_full, 1)

            def max_turn(l, i, g):
                after(pe, row_free, row_use(l, i, "shift", g))
                nc.tensor.transpose(rows[:, 0, 0:S], mx[:], ident[0:S, 0:S]).then_inc(row_full, 1)

            def context_turn(l, i):
                pe.wait_ge(ctx_chain, i * 6 + (6 * (l * B + 1) + 1))
                after(pe, row_free, row_use(l, i, "cmax", G - 1))
                nc.tensor.transpose(rows[:, 0, 0:P], cs[:, 0:1].to_broadcast([P, P]), ident).then_inc(row_full, 1)

            def score_tile(l, i, g, j):
                t = step(l, i, g)
                if j == 0:
                    after(pe, q_low, t + 1)
                    pe.wait_ge(k_low, 2 * t + 2)
                    pe.wait_ge(kt_low, i + (l * B + 1))
                after(pe, p_high, t * NT + max(j - 1, 0))
                n = KEY if j else TP
                out = st[0:n, j % 2, 0:Q4]
                hi = k_hi[:, g % 2, (j - 1) * KEY:j * KEY] if j else kt_hi[:, g, :]
                lo = k_lo[:, g % 2, (j - 1) * KEY:j * KEY] if j else kt_lo[:, g, :]
                nc.tensor.matmul(out, hi, q_hi[:, :, :], start=True, stop=False)
                nc.tensor.matmul(out, hi, q_lo[:, :, :], start=False, stop=False)
                nc.tensor.matmul(out, lo, q_hi[:, :, :], start=False, stop=False)
                if j == 0:
                    after(pe, row_free, row_use(l, i, "shift", g) + 1)
                nc.tensor.matmul(out, sel[:, min(j, 1), 0:n], shift[:, :, :], start=False, stop=True).then_inc(s_full, 1)

            def weigh(l, i, g):
                t = step(l, i, g)
                after(pe, p_low, t * NT + NT)
                after(pe, v_parts, 2 * t + 2)
                after(pe, pv_read, t)
                for h in range(HG):
                    for part, tiles in ((0, (0,)), (1, range(1, NT))):
                        for j in tiles:
                            n = TEXT if j == 0 else LAST if j == NT - 1 else KEY
                            for m, p in enumerate((p_hi, p_lo)):
                                mm = nc.tensor.matmul(pv[:, part, h * VS:(h + 1) * VS], p[0:n, j, h * S:h * S + P],
                                                      vst[0:n, g % 2, j, h, :], start=(j == tiles[0] and m == 0),
                                                      stop=(j == tiles[-1] and m == 1))
                mm.then_inc(pv_full, 1)

            def o_turn(l, i, g):
                pe.wait_ge(o_sum, step(l, i, g) + 1)
                after(pe, row_free, row_use(l, i, "oT", g))
                nc.tensor.transpose(rows[:, 0, 0:S], acc[:, 0].rearrange("s h d -> s (h d)"),
                                    ident[0:S, 0:S]).then_inc(row_full, 1)

            def project(l, i, g):
                return (lambda: k_unit(l, i, g, 0), lambda: k_unit(l, i, g, 1), lambda: v_unit(l, i, g, 0),
                        lambda: v_unit(l, i, g, 1), lambda: v_turn(l, i, g, 0), lambda: v_turn(l, i, g, 1))

            def nothing():
                return (lambda: None,) * 6

            pe.wait_ge(const_in, 64)
            for half in range(2):
                q_half(0, half)
            for l in range(LAYERS):
                pe.wait_ge(w_low, 8 * (l + 1))
                pe.wait_ge(q_evac, 2 * CT * (l + 1))
                pe.wait_ge(sel_ok, 2)
                pe.wait_ge(pads, l + 1)
                with pe.Fori(0, B) as i:
                    k_text(l, i)
                    k0, k1, v0, v1, t0, t1 = project(l, i, 0)
                    if l:
                        after(pe, qrow_ok, i + (l * B + 1))
                        after(pe, row_free, row_use(l, i, "logit"))
                        for g in range(G):
                            mm = nc.tensor.matmul(rows[0:S, 0, 0:TP], q_row[:, g, :], kt32[:, g, :],
                                                  start=(g == 0), stop=(g == G - 1))
                        mm.then_inc(row_full, 1)
                        k0()
                        pe.wait_ge(probs, i * 5 + 5)
                        after(pe, row_free, row_use(l, i, "pT"))
                        nc.tensor.transpose(rows[:, 0, 0:S], mx[:], ident[0:S, 0:S]).then_inc(row_full, 1)
                        k1()
                        after(pe, row_free, row_use(l, i, "ti"))
                        for c in range(2):
                            mm = pairs(rows[0:TP, c, 0:HALF], tokens(0, TP),
                                       tokens(TP + c * HALF, TP + (c + 1) * HALF), KT)
                        mm.then_inc(row_full, 1)
                        v0()
                        after(pe, row_free, row_use(l, i, "semq"))
                        for c in range(2):
                            mm = nc.tensor.matmul(rows[0:S, c, 0:HALF], pT[:], ti[0:TEXT, c, :], start=True, stop=True)
                        mm.then_inc(row_full, 1)
                        v1()
                        after(pe, row_free, row_use(l, i, "semk"))
                        tif = ti[0:TEXT].rearrange("p c t -> p (c t)")
                        for j in range(NIP):
                            mm = nc.tensor.matmul(rows[0:KEY, j // 3, j % 3 * S:(j % 3 + 1) * S],
                                                  tif[:, j * KEY:(j + 1) * KEY], pT[:], start=True, stop=True)
                        mm.then_inc(row_full, 1)
                    else:
                        k0(), k1(), v0(), v1()
                    t0(), t1()
                    for g in range(G):
                        k0, k1, v0, v1, t0, t1 = project(l, i, g + 1) if g < G - 1 else nothing()
                        max_scores(l, i, g, 0)
                        k0()
                        if g:
                            o_turn(l, i, g - 1)
                        max_scores(l, i, g, 1)
                        k1()
                        max_scores(l, i, g, 2)
                        max_scores(l, i, g, 3)
                        v0()
                        max_turn(l, i, g)
                        score_tile(l, i, g, 0)
                        score_tile(l, i, g, 1)
                        v1()
                        if g == G - 1:
                            context_turn(l, i)
                        for j in (2, 3, 4):
                            score_tile(l, i, g, j)
                        t0()
                        score_tile(l, i, g, 5)
                        t1()
                        score_tile(l, i, g, 6)
                        weigh(l, i, g)
                    o_turn(l, i, G - 1)
                after(pe, row_free, row_use(l, B - 1, "oT", G - 1) + 1)
                out_phase(l)

        @block.scalar
        def _(act):
            def load_weight(l, w):
                if w or l:
                    act.wait_ge(w_low, 2 * (4 * l + w))
                if l and w == 0:
                    after(act, pv_full, l * STEPS)
                act.dma_start(w_raw, w_d[l * 4 + w]).then_inc(w_in, 16)

            def split_weight(l, w):
                act.wait_ge(w_chain, 6 * (4 * l + w) + 6)
                for n in range(2):
                    a, b = n * KT // 2, (n + 1) * KT // 2
                    nc.scalar.activation(w_hi[:, w, a:b, :].rearrange("p k c -> p (k c)"), w_raw[:, a * C:b * C],
                                         ACT.Copy, scale=wscale[:, w:w + 1]).then_inc(w_high, 1)

            def split_context(n, k):
                nc.scalar.activation(c_hi[:, k, :], ctx_raw[:, k, :], ACT.Copy, scale=cs[:, 4:5]).then_inc(ctx_high, 1)

            def q_half(l, half):
                for c in range(CT):
                    n = (CT * half + c) if l == 0 else 2 * CT + 2 * CT * half + CT + c
                    act.wait_ge(lin_full, n + 1)
                    nc.scalar.activation(qo[:, c, half * MT:(half + 1) * MT], banks[n % 2][:, 0:MT],
                                         ACT.Copy).then_inc(q_evac, 1)

            def k_text(l, i):
                act.wait_ge(inv_ok, i + (l * B + 1))
                act.wait_ge(row_full, row_use(l, i, "kt") + 1)
                after(act, s_full, i * G * NT + l * STEPS * NT)
                nc.scalar.activation(kt32[:].rearrange("p g t -> p (g t)"), rows[:, 0, 0:G * TP], ACT.Copy,
                                     scale=inv[:, 0:1]).then_inc(row_free, 1)
                after(act, row_free, row_use(l, i, "kt") + 1)
                nc.scalar.activation(kt_hi[:], kt32[:], ACT.Copy).then_inc(kt_high, 1)

            def k_unit(l, i, g, c):
                u = step(l, i, g)
                act.wait_ge(k_full, 2 * u + (c + 1))
                after(act, s_full, (u if g == 0 else u - 1) * NT)
                nc.scalar.activation(k_hi[:, g % 2, c * HALF:(c + 1) * HALF], banks[c][:, 0:HALF], ACT.Copy,
                                     scale=inv[:, 1:2]).then_inc(k_high, 1)

            def v_unit(l, i, g, c):
                u = step(l, i, g)
                act.wait_ge(v_full, 2 * u + (c + 1))
                after(act, vt_full, 2 * u)
                if c == 0:
                    nc.scalar.activation(vT[:, 0:TP], bankA[:, 0:TP], ACT.Copy, scale=inv[:, 2:3])
                    last = nc.scalar.activation(vT[:, TP:TP + HALF], bankA[:, TP:TP + HALF], ACT.Copy, scale=inv[:, 3:4])
                else:
                    last = nc.scalar.activation(vT[:, TP + HALF:TOKP], bankB[:, 0:HALF], ACT.Copy, scale=inv[:, 3:4])
                last.then_inc(vT_ok, 1)

            def v_turn(l, i, g, c):
                u = step(l, i, g)
                after(act, vt_full, 2 * u + (c + 1))
                after(act, pv_full, u if g == 0 else u - 1)
                a, b = (0, 4) if c == 0 else (4, NT)
                for t in range(a, b):
                    last = nc.scalar.activation(vst[0:KEY, g % 2, t, :, 0:D],
                                                banks[c][0:KEY, (t - a) * P:(t - a + 1) * P].rearrange("p (h d) -> p h d", h=HG),
                                                ACT.Copy)
                last.then_inc(v_high, 1)

            def q_high_part(l, i, g):
                t = step(l, i, g)
                act.wait_ge(qbd_ok, t + 1)
                after(act, s_full, t * NT)
                nc.scalar.activation(q_hi[:], qbd[:], ACT.Copy).then_inc(q_high, 1)

            def exps(l, i, g, j):
                t = step(l, i, g)
                if l and j:
                    act.wait_ge(sadd, (t - STEPS) * NIP + j)
                    src = prob[0:KEY, j % 3, :]
                else:
                    after(act, s_full, t * NT + (j + 1))
                    src = st[0:KEY if j else TP, j % 2, 0:Q4]
                if j == 0:
                    after(act, pv_full, t)
                after(act, p_low, t * NT + (j - 2 if j >= 3 else 0))
                n = KEY if j else TP
                nc.scalar.activation(p_hi[0:n, j, 0:Q4], src, ACT.Exp, scale=SC)
                nc.scalar.activation(prob[0:n, j % 3, :], src, ACT.Exp, scale=SC).then_inc(p_high, 1)

            def o_turn(l, i, g):
                act.wait_ge(row_full, row_use(l, i, "oT", g) + 1)
                nc.scalar.activation(qo[:, g, bass.ds(i * S, S)], rows[:, 0, 0:S], ACT.Copy).then_inc(row_free, 1)

            def project(l, i, g):
                return (lambda: k_unit(l, i, g, 0), lambda: k_unit(l, i, g, 1), lambda: v_unit(l, i, g, 0),
                        lambda: v_unit(l, i, g, 1), lambda: v_turn(l, i, g, 0), lambda: v_turn(l, i, g, 1))

            def nothing():
                return (lambda: None,) * 6

            load_weight(0, 0)
            act.wait_ge(ctx_chain, 6)
            for k in range(KT):
                split_context(0, k)
            for w in range(4):
                split_weight(0, w)
                if w < 3:
                    load_weight(0, w + 1)
                if w == 0:
                    q_half(0, 0)
                if w == 1:
                    q_half(0, 1)
            for l in range(LAYERS):
                with act.Fori(0, B) as i:
                    k_text(l, i)
                    if l:
                        act.wait_ge(probs, i * 5 + 2)
                        nc.scalar.activation(mx[:, 0:TEXT], rows[0:S, 0, 0:TEXT], ACT.Exp, bias=sm[:, 1:2],
                                             scale=SC).then_inc(row_free, 1)
                    for unit in project(l, i, 0):
                        unit()
                    for g in range(G):
                        k0, k1, v0, v1, t0, t1 = project(l, i, g + 1) if g < G - 1 else nothing()
                        q_high_part(l, i, g)
                        k0()
                        if g:
                            o_turn(l, i, g - 1)
                        k1()
                        v0()
                        if g == G - 1:
                            act.wait_ge(ctx_chain, i * 6 + 6 * (l * B + 2))
                        for j in range(NT):
                            exps(l, i, g, j)
                            if j == 1:
                                v1()
                            if j == 4:
                                t0()
                            if j == 5:
                                t1()
                            if g == G - 1:
                                split_context(None, j)
                        if g == G - 1:
                            split_context(None, NT)
                    o_turn(l, i, G - 1)
                if l == 0:
                    load_weight(1, 0)
                    q_half(1, 0)
                    split_weight(1, 0)
                    load_weight(1, 1)
                    split_weight(1, 1)
                    load_weight(1, 2)
                    q_half(1, 1)
                    split_weight(1, 2)
                    load_weight(1, 3)
                    split_weight(1, 3)

        @block.gpsimd
        def _(pool):
            def all_max(ap, chain, n):
                pool.wait_ge(chain, n)
                nc.gpsimd.partition_all_reduce(ap[:, 1:2], ap[:, 0:1], P, RMAX).then_inc(chain, 1)

            def ones_and_pads(l):
                for b in range(2):
                    nc.gpsimd.memset(vst[:, b, :, :, 3 * D:VS].rearrange("p t h v -> p (t h) v"), 1.0)
                for p in (p_hi, p_lo):
                    last = nc.gpsimd.memset(p[:, :, Q4:PW], 0.0)
                last.then_inc(pads, 1)

            def q_spread(l, i, g):
                t = step(l, i, g)
                if g == 0:
                    after(pool, q_low, t)
                    nc.gpsimd.tensor_copy(q_row[:], qo[:, :, bass.ds(i * S, S)]).then_inc(qrow_ok, 1)
                    after(pool, qrow_ok, i + (l * B + 1))
                after(pool, q_low, t)
                nc.gpsimd.tensor_tensor(qbd[:], q_row[:, g, :].unsqueeze(1).to_broadcast([P, HG, S]),
                                        hmask.unsqueeze(2).to_broadcast([P, HG, S]), ALU.mult).then_inc(qbd_ok, 1)

            def v_turn(l, i, g, c):
                u = step(l, i, g)
                after(pool, v_res, 2 * u + (c + 1))
                a, b = (0, 4) if c == 0 else (4, NT)
                rest = v_rest[0:KEY, 0:(b - a) * P].rearrange("p (t h d) -> p t h d", t=b - a, h=HG)
                one = ones[0:KEY].unsqueeze(2).to_broadcast([KEY, HG, D])
                for t in range(a, b):
                    last = nc.gpsimd.tensor_tensor(vst[0:KEY, g % 2, t, :, D:2 * D], rest[:, t - a], one, ALU.mult)
                last.then_inc(v_mid, 1)
                pool.wait_ge(v_mid, 2 * u + (c + 1))
                for t in range(a, b):
                    last = nc.gpsimd.tensor_tensor(vst[0:KEY, g % 2, t, :, 2 * D:3 * D], rest[:, t - a],
                                                   vst[0:KEY, g % 2, t, :, D:2 * D], ALU.subtract)
                last.then_inc(v_parts, 1)

            for n, s in enumerate(PRIMED):
                nc.gpsimd.memset(primer[:, n:n + 1], 0.0).then_inc(s, 1)
            all_max(cs, ctx_chain, 1)
            for l in range(LAYERS):
                for w in range(4):
                    all_max(ws, w_chain, 6 * (4 * l + w) + 1)
                pool.wait_ge(w_low, 8 * (l + 1))
                pool.wait_ge(sel_ok, 2)
                if l:
                    pool.wait_ge(out_evac, 2 * CT)
                ones_and_pads(l)
                pool.wait_ge(q_evac, 2 * CT * (l + 1))
                with pool.Fori(0, B) as i:
                    q_spread(l, i, 0)
                    v_turn(l, i, 0, 0)
                    v_turn(l, i, 0, 1)
                    for g in range(G):
                        if g < G - 1:
                            v_turn(l, i, g + 1, 0)
                            v_turn(l, i, g + 1, 1)
                            q_spread(l, i, g + 1)

        @block.vector
        def _(dve):
            def scale_chain(ap, chain, base, s_out, inv_out):
                dve.wait_ge(chain, base + 2)
                nc.vector.tensor_scalar(ap[:, 2:3], ap[:, 1:2], TINY, None, ALU.max).then_inc(chain, 1)
                dve.wait_ge(chain, base + 3)
                nc.vector.tensor_scalar(ap[:, 3:4].bitcast(I32), ap[:, 2:3].bitcast(I32), EXP_BITS, None,
                                        ALU.bitwise_and).then_inc(chain, 1)
                dve.wait_ge(chain, base + 4)
                nc.vector.tensor_scalar(inv_out, ap[:, 3:4], 1.0 / TOP, None, ALU.mult).then_inc(chain, 1)
                dve.wait_ge(chain, base + 5)
                nc.vector.reciprocal(s_out, inv_out).then_inc(chain, 1)

            def weight(l, w):
                n = 4 * l + w
                dve.wait_ge(w_in, 16 * (n + 1))
                nc.vector.tensor_reduce(ws[:, 0:1], w_raw, AX.X, ALU.max, apply_absolute_value=True).then_inc(w_chain, 1)
                scale_chain(ws, w_chain, 6 * n, wscale[:, w:w + 1], winv[:, w:w + 1])
                for m in range(2):
                    a, b = m * KT // 2, (m + 1) * KT // 2
                    dve.wait_ge(w_high, 2 * n + m + 1)
                    nc.vector.scalar_tensor_tensor(w_lo[:, w, a:b, :].rearrange("p k c -> p (k c)"), w_raw[:, a * C:b * C],
                                                   wscale[:, w:w + 1], w_hi[:, w, a:b, :].rearrange("p k c -> p (k c)"),
                                                   ALU.mult, ALU.subtract).then_inc(w_low, 1)

            def context_max(n):
                dve.wait_ge(ctx_in, n * 16 + 16)
                nc.vector.tensor_reduce(cs[:, 0:1], raw[:], AX.X, ALU.max, apply_absolute_value=True).then_inc(ctx_chain, 1)

            def context_turn(l, i):
                dve.wait_ge(row_full, row_use(l, i, "cmax", G - 1) + 1)
                nc.vector.tensor_reduce(cs[:, 1:2], rows[:, 0, 0:P], AX.X, ALU.max).then_inc(ctx_chain, 1)
                dve.wait_ge(ctx_chain, i * 6 + (6 * (l * B + 1) + 2))
                nc.vector.tensor_copy(cs[:, 6:7], cs[:, 1:2]).then_inc(row_free, 1)

            def context_scale(n):
                scale_chain(cs, ctx_chain, n * 6, cs[:, 4:5], cs[:, 5:6])

            def split_context(n, k):
                dve.wait_ge(ctx_high, n * KT + (k + 1))
                nc.vector.scalar_tensor_tensor(c_lo[:, k, :], ctx_raw[:, k, :], cs[:, 4:5], c_hi[:, k, :],
                                               ALU.mult, ALU.subtract).then_inc(ctx_low, 1)

            def out_half(l, half):
                dve.wait_ge(xh_in, 16 * (2 * (l + 1) + half + 1))
                for c in range(CT):
                    n = 2 * CT + (2 * CT * half if l == 0 else 4 * CT + CT * half) + c
                    dve.wait_ge(lin_full, n + 1)
                    nc.vector.scalar_tensor_tensor(xh[:, c, :], banks[n % 2][:, 0:MT], bias[:, l, c:c + 1], xh[:, c, :],
                                                   ALU.add, ALU.add).then_inc(out_evac, 1)

            def k_text(l, i):
                dve.wait_ge(kt_high, i + (l * B + 1))
                nc.vector.tensor_tensor(kt_lo[:], kt32[:], kt_hi[:].bitcast(F32), ALU.subtract).then_inc(kt_low, 1)

            def k_unit(l, i, g, c):
                u = step(l, i, g)
                dve.wait_ge(k_high, 2 * u + (c + 1))
                a, b = c * HALF, (c + 1) * HALF
                nc.vector.scalar_tensor_tensor(k_lo[:, g % 2, a:b], banks[c][:, 0:HALF], inv[:, 1:2],
                                               k_hi[:, g % 2, a:b].bitcast(F32), ALU.mult, ALU.subtract).then_inc(k_low, 1)

            def v_turn(l, i, g, c):
                u = step(l, i, g)
                dve.wait_ge(v_high, 2 * u + (c + 1))
                after(dve, v_parts, 2 * u + c)
                a, b = (0, 4) if c == 0 else (4, NT)
                n = b - a
                nc.vector.tensor_tensor(v_rest[0:KEY, 0:n * P].rearrange("p (n d) -> p n d", d=D),
                                        banks[c][0:KEY, 0:n * P].rearrange("p (n d) -> p n d", d=D),
                                        vst[0:KEY, g % 2, a:b, :, 0:D].rearrange("p t h d -> p (t h) d"),
                                        ALU.subtract).then_inc(v_res, 1)

            def q_low_part(l, i, g):
                dve.wait_ge(q_high, step(l, i, g) + 1)
                nc.vector.tensor_tensor(q_lo[:], qbd[:], q_hi[:].bitcast(F32), ALU.subtract).then_inc(q_low, 1)

            def maxima(l, i, g, h):
                dve.wait_ge(row_full, row_use(l, i, f"max{h}", g) + 1)
                nc.vector.tensor_reduce(mx[:, h:h + 1], rows[0:S, 0, HALF:HALF + TP], AX.X, ALU.max)
                if l:
                    last = nc.vector.tensor_tensor_reduce(out=ti[0:S], in0=rows[0:S, :, 0:HALF], in1=semq[:], scale=1.0,
                                                          scalar=LOWEST, op0=ALU.add, op1=ALU.max,
                                                          accum_out=mx[:, HG + h:HG + h + 1])
                else:
                    last = nc.vector.tensor_reduce(mx[:, HG + h:HG + h + 1], rows[0:S, :, 0:HALF], AX.XY, ALU.max)
                last.then_inc(row_free, 1)

            def shift_build(l, i, g):
                dve.wait_ge(row_full, row_use(l, i, "shift", g) + 1)
                after(dve, s_full, step(l, i, g) * NT)
                nc.vector.tensor_tensor(shift[:], rows[:, 0, 0:S].unsqueeze(1).to_broadcast([P, HG, S]),
                                        nmask.unsqueeze(2).to_broadcast([P, HG, S]), ALU.mult).then_inc(row_free, 1)

            def add_semantic(l, i, g, j):
                t = step(l, i, g)
                after(dve, s_full, t * NT + (j + 1))
                after(dve, p_low, t * NT + (j - 2 if j >= 3 else 0))
                nc.vector.tensor_tensor(prob[0:KEY, j % 3, :].rearrange("p (h q) -> p h q", h=HG),
                                        st[0:KEY, j % 2, 0:Q4].rearrange("p (h q) -> p h q", h=HG),
                                        semk[:, j - 1, :].unsqueeze(1).to_broadcast([KEY, HG, S]),
                                        ALU.add).then_inc(sadd, 1)

            def prob_low(l, i, g, j):
                t = step(l, i, g)
                after(dve, p_high, t * NT + (j + 1))
                n = KEY if j else TP
                nc.vector.tensor_tensor(p_lo[0:n, j, 0:Q4], prob[0:n, j % 3, :], p_hi[0:n, j, 0:Q4],
                                        ALU.subtract).then_inc(p_low, 1)

            def normalise(l, i, g):
                t = step(l, i, g)
                after(dve, pv_full, t + 1)
                out = pv[0:S, :, 0:HG * VS].rearrange("s b (h v) -> s b h v", h=HG)
                nc.vector.reciprocal(den[:], out[:, :, :, 3 * D]).then_inc(norm, 1)
                for b in range(2):
                    nc.vector.tensor_reduce(acc[:, b], out[:, b, :, 0:3 * D].rearrange("s h (m d) -> s h d m", m=3),
                                            AX.X, ALU.add).then_inc(pv_read if b else norm, 1)
                dve.wait_ge(norm, t * 4 + 1)
                nc.vector.tensor_scalar(den[:, 1, :], den[:, 1, :], mask[:, l:l + 1], None, ALU.mult).then_inc(norm, 1)
                dve.wait_ge(norm, t * 4 + 3)
                after(dve, pv_read, t + 1)
                nc.vector.tensor_tensor(acc[:], acc[:], den[:].unsqueeze(3).to_broadcast([S, 2, HG, D]),
                                        ALU.mult).then_inc(norm, 1)
                dve.wait_ge(norm, t * 4 + 4)
                nc.vector.tensor_tensor(acc[:, 0], acc[:, 0], acc[:, 1], ALU.add).then_inc(o_sum, 1)

            def project(l, i, g):
                return (lambda: k_unit(l, i, g, 0), lambda: k_unit(l, i, g, 1), lambda: v_turn(l, i, g, 0),
                        lambda: v_turn(l, i, g, 1))

            dve.wait_ge(const_in, 64)
            nc.vector.tensor_copy(sel[:].rearrange("p a k -> p (a k)"), sel_raw).then_inc(sel_ok, 1)
            nc.vector.memset(mx[:], 0.0).then_inc(sel_ok, 1)
            context_max(0)
            context_scale(0)
            for k in range(KT):
                split_context(0, k)
            for l in range(LAYERS):
                for w in range(4):
                    if l and w % 2 == 0:
                        out_half(0, w // 2)
                    weight(l, w)
                dve.wait_ge(w_chain, 24 * (l + 1))
                with dve.Fori(0, B) as i:
                    nc.vector.tensor_scalar(inv[:], winv[:], cs[:, 5:6], None, ALU.mult).then_inc(inv_ok, 1)
                    k_text(l, i)
                    k0, k1, t0, t1 = project(l, i, 0)
                    dve.wait_ge(inv_ok, i + (l * B + 1))
                    if l:
                        dve.wait_ge(row_full, row_use(l, i, "logit") + 1)
                        nc.vector.tensor_reduce(sm[:, 0:1], rows[0:S, 0, 0:TEXT], AX.X, ALU.max).then_inc(probs, 1)
                        dve.wait_ge(probs, i * 5 + 1)
                        nc.vector.tensor_scalar(sm[:, 1:2], sm[:, 0:1], -SC, None, ALU.mult).then_inc(probs, 1)
                        k0()
                        after(dve, row_free, row_use(l, i, "logit") + 1)
                        nc.vector.tensor_reduce(sm[:, 2:3], mx[:, 0:TEXT], AX.X, ALU.add).then_inc(probs, 1)
                        dve.wait_ge(probs, i * 5 + 3)
                        nc.vector.reciprocal(sm[:, 3:4], sm[:, 2:3]).then_inc(probs, 1)
                        dve.wait_ge(probs, i * 5 + 4)
                        nc.vector.tensor_scalar(mx[:, 0:TEXT], mx[:, 0:TEXT], sm[:, 3:4], None, ALU.mult).then_inc(probs, 1)
                        dve.wait_ge(row_full, row_use(l, i, "pT") + 1)
                        nc.vector.tensor_copy(pT[:], rows[0:TEXT, 0, 0:S]).then_inc(row_free, 1)
                        k1()
                        dve.wait_ge(row_full, row_use(l, i, "ti") + 1)
                        nc.vector.tensor_scalar(ti[0:TP], rows[0:TP, :, 0:HALF], cs[0:TP, 5:6], cs[0:TP, 5:6],
                                                ALU.mult, ALU.mult).then_inc(row_free, 1)
                        dve.wait_ge(row_full, row_use(l, i, "semq") + 1)
                        nc.vector.tensor_scalar(semq[:], rows[0:S, :, 0:HALF], SEM, None, ALU.mult).then_inc(row_free, 1)
                        dve.wait_ge(row_full, row_use(l, i, "semk") + 1)
                        nc.vector.tensor_scalar(semk[:].rearrange("p (b t) q -> p b (t q)", b=2),
                                                rows[0:KEY, :, 0:NIP // 2 * S], SEM, None, ALU.mult).then_inc(row_free, 1)
                    else:
                        k0(), k1()
                    t0(), t1()
                    for g in range(G):
                        k0, k1, t0, t1 = project(l, i, g + 1) if g < G - 1 else (lambda: None,) * 4
                        q_low_part(l, i, g)
                        maxima(l, i, g, 0)
                        k0()
                        maxima(l, i, g, 1)
                        k1()
                        maxima(l, i, g, 2)
                        maxima(l, i, g, 3)
                        shift_build(l, i, g)
                        if g == G - 1:
                            context_turn(l, i)
                            context_scale(i + (l * B + 1))
                        for j in range(NT):
                            if l and j < NT - 1:
                                add_semantic(l, i, g, j + 1)
                            prob_low(l, i, g, j)
                            if j == 4:
                                t0()
                            if j == 5:
                                t1()
                            if g == G - 1:
                                split_context(i + (l * B + 1), j)
                        if g == G - 1:
                            split_context(i + (l * B + 1), NT)
                        if g == G - 2:
                            context_max(i + (l * B + 1))
                        normalise(l, i, g)
            for half in range(2):
                out_half(1, half)


def kernel(x, ctx_2048, fside_S_0, L0_xattn_Wq, L0_xattn_Wk, L0_xattn_Wv, L0_xattn_Wk_ip, L0_xattn_Wv_ip,
           L0_xattn_Wo, L0_xattn_bo, L1_xattn_Wq, L1_xattn_Wk, L1_xattn_Wv, L1_xattn_Wk_ip, L1_xattn_Wv_ip,
           L1_xattn_Wout, L1_xattn_bout):
    import concourse.bacc as bacc
    from concourse.bass_utils import run_bass_kernel_spmd

    def rows_first(w):
        w = np.asarray(w)
        return w.reshape(-1, P, w.shape[1]).transpose(1, 0, 2).reshape(P, -1)

    ctx = np.asarray(ctx_2048)
    order = list(range(TEXT)) + [TEXT - 1] + list(range(TEXT, TOK)) + [TOK - 1] * (IPP - IP)
    ctx = ctx[:, order, :].transpose(0, 2, 1).reshape(B, KT, P, TOKP).transpose(0, 2, 1, 3).reshape(B, P, KT * TOKP)
    ctx = np.concatenate([ctx, ctx[:1]])
    xs = np.asarray(x).reshape(2, MT, CT, P).transpose(0, 3, 2, 1)
    weights = [np.asarray(w).T for w in (L0_xattn_Wk, L0_xattn_Wk_ip, L0_xattn_Wv, L0_xattn_Wv_ip)]
    weights += [np.asarray(w) for w in (L1_xattn_Wk, L1_xattn_Wk_ip, L1_xattn_Wv, L1_xattn_Wv_ip)]
    const = np.zeros((P, P + 3 * HG + 2 * KEY), np.float32)
    const[:, 0:P] = np.eye(P)
    const[:, P + 2 * HG:P + 3 * HG] = 1.0
    const[0:HG, P + 3 * HG:P + 3 * HG + KEY] = 1.0
    const[HG:2 * HG, P + 3 * HG + KEY:] = 1.0
    for h in range(HG):
        const[h * D:(h + 1) * D, P + h] = 1.0
        const[[h, HG + h], P + HG + h] = -1.0
    arrays = {
        "ctx": ctx,
        "x": xs,
        "w": np.stack([rows_first(w) for w in weights]),
        "wq": np.stack([rows_first(np.asarray(L0_xattn_Wq).T), rows_first(L1_xattn_Wq)]).reshape(LAYERS, P, CT, C),
        "wo": np.stack([rows_first(np.asarray(L0_xattn_Wo).T), rows_first(L1_xattn_Wout)]).reshape(LAYERS, P, CT, C),
        "bias": np.stack([np.asarray(b).reshape(CT, P).T for b in (L0_xattn_bo, L1_xattn_bout)], axis=1),
        "mask": np.stack([np.ones(S, np.float32), np.asarray(fside_S_0)], axis=1),
        "const": const,
    }
    arrays = {f"{n}_dram": np.ascontiguousarray(a) for n, a in arrays.items()}
    nc = bacc.Bacc("TRN2", target_bir_lowering=False, num_devices=1)
    ins = [nc.dram_tensor(n, a.shape, mybir.dt.from_np(a.dtype), kind="ExternalInput").ap() for n, a in arrays.items()]
    x1 = nc.dram_tensor("x1_dram", (2, P, CT, MT), F32, kind="Internal").ap()
    out = nc.dram_tensor("out_dram", (2, P, CT, MT), F32, kind="ExternalOutput").ap()
    xattn_pair_kernel(nc, *ins, x1, out)
    got = run_bass_kernel_spmd(nc, [arrays], core_ids=[0]).results[0]["out_dram"]
    return got.transpose(0, 3, 2, 1).reshape(B, S, C)
```

```python
from contextlib import ExitStack

import concourse.bass as bass
import numpy as np
from concourse import mybir

ALU = mybir.AluOpType
ACT = mybir.ActivationFunctionType
AX = mybir.AxisListType
F32 = mybir.dt.float32
F32R = mybir.dt.float32r
F16 = mybir.dt.float16
BF16 = mybir.dt.bfloat16
I32 = mybir.dt.int32
RMAX = bass.bass_isa.ReduceOp.max

P = 128
B, S, C, CC = 8, 100, 640, 1024
TOK = 722
H, D = 20, 32
TEXT = 77
IP = TOK - TEXT
LAYERS = 2
HG = P // D
G = H // HG
KT = CC // P
CT = C // P
KEY = 108
NIP = -(-IP // KEY)
NT = 1 + NIP
TP = TEXT + 1
IPP = KEY * NIP
HALF = IPP // 2
LAST = IP - KEY * (NIP - 1)
TOKP = TP + IPP
Q4 = HG * S
VS = 3 * D + 2
PW = Q4 + 32
MT = B * S // 2
STEPS = B * G
SC = float(D) ** -0.5
SEM = 0.5
TINY = 1e-30
TOP = 2.0 ** 14
EXP_BITS = 0x7F800000
LOWEST = -3.0e38


def xattn_pair_kernel(nc, ctx_d, x_d, w_d, wq_d, wo_d, bias_d, mask_d, const_d, x1_d, out_d):
    with ExitStack() as stack:
        def sb(name, shape, dt):
            return stack.enter_context(nc.sbuf_tensor(name, shape, dt))

        def psum(name, shape, dt=F32):
            return stack.enter_context(nc.psum_tensor(name, shape, dt))

        def sem(name):
            return stack.enter_context(nc.semaphore(name))

        w_hi = sb("w_hi", [P, 4, KT, C], F16)
        w_lo = sb("w_lo", [P, 4, KT, C], F16)
        c_hi = sb("c_hi", [P, KT, TOKP], F16)
        c_lo = sb("c_lo", [P, KT, TOKP], F16)
        raw = sb("raw", [P, KT * TOKP], F32)
        ctx_raw = raw[:, :].rearrange("p (k t) -> p k t", k=KT)
        xh = raw[:, 0:CT * MT].rearrange("p (c t) -> p c t", c=CT)
        wq = raw[:, CT * MT:CT * MT + CT * C].rearrange("p (k n) -> p k n", k=CT)
        qo = sb("qo", [P, CT, B * S], F32)
        work = sb("work", [P, 2744 + TOKP + 512 + 3 * Q4], F32)
        w_raw = work[:, 0:KT * C]
        vst = work[:, 0:2744].bitcast(BF16).rearrange("p (b t h v) -> p b t h v", b=2, t=NT, h=HG)
        vT = work[:, 2744:2744 + TOKP]
        v_rest = work[:, 2744 + TOKP:2744 + TOKP + 512]
        prob = work[:, 2744 + TOKP + 512:2744 + TOKP + 512 + 3 * Q4].rearrange("p (r q) -> p r q", r=3)
        pwork = sb("pwork", [P, CT * C], F32)
        wo = pwork[:, :].rearrange("p (k n) -> p k n", k=CT)
        sel_raw = pwork[:, 0:2 * KEY]
        p_hi = pwork[:, 0:NT * PW // 2].bitcast(F16).rearrange("p (t q) -> p t q", t=NT)
        p_lo = pwork[:, NT * PW // 2:NT * PW].bitcast(F16).rearrange("p (t q) -> p t q", t=NT)
        k_hi = sb("k_hi", [P, 2, IPP], F32R)
        k_lo = sb("k_lo", [P, 2, IPP], F32R)
        kt32 = sb("kt32", [P, G, TP], F32)
        kt_hi = sb("kt_hi", [P, G, TP], F32R)
        kt_lo = sb("kt_lo", [P, G, TP], F32R)
        q_row = sb("q_row", [P, CT, S], F32)
        qbd = sb("qbd", [P, HG, S], F32)
        q_hi = sb("q_hi", [P, HG, S], F32R)
        q_lo = sb("q_lo", [P, HG, S], F32R)
        shift = sb("shift", [P, HG, S], F32R)
        sel = sb("sel", [P, 2, KEY], F32R)
        const = sb("const", [P, P + 3 * HG], F32)
        ident = const[:, 0:P]
        hmask = const[:, P:P + HG]
        nmask = const[:, P + HG:P + 2 * HG]
        ones = const[:, P + 2 * HG:P + 3 * HG]
        bias = sb("bias", [P, LAYERS, CT], F32)
        mask = sb("mask", [S, LAYERS], F32)
        mx = sb("mx", [S, P], F32)
        semq = sb("semq", [S, 2, HALF], F32)
        semk = sb("semk", [KEY, NIP, S], F32)
        ti = sb("ti", [P, 2, HALF], F32)
        pT = sb("pT", [TEXT, S], F32)
        acc = sb("acc", [S, 2, HG, D], F32)
        den = sb("den", [S, 2, HG], F32)
        wscale = sb("wscale", [P, 4], F32)
        winv = sb("winv", [P, 4], F32)
        cs = sb("cs", [P, 8], F32)
        cparts = sb("cparts", [P, KT], F32)
        ws = sb("ws", [P, 4], F32)
        inv = sb("inv", [P, 4], F32)
        sm = sb("sm", [S, 4], F32)
        primer = sb("primer", [1, 16], F32)

        bankA, bankB = psum("bankA", [P, 512]), psum("bankB", [P, 512])
        rows = psum("rows", [P, 2, 512])
        st = psum("st", [P, 2, 512])
        pv = psum("pv", [P, 2, 512])
        banks = (bankA, bankB)

        const_in, sel_ok = sem("const_in"), sem("sel_ok")
        w_in, w_chain, w_high, w_low = sem("w_in"), sem("w_chain"), sem("w_high"), sem("w_low")
        ctx_parts = sem("ctx_parts")
        ctx_in, ctx_chain, ctx_high, ctx_low = sem("ctx_in"), sem("ctx_chain"), sem("ctx_high"), sem("ctx_low")
        wq_in, wo_in, xh_in = sem("wq_in"), sem("wo_in"), sem("xh_in")
        x1_out, y_out = sem("x1_out"), sem("y_out")
        lin_full, q_evac, out_evac = sem("lin_full"), sem("q_evac"), sem("out_evac")
        row_full, row_free = sem("row_full"), sem("row_free")
        kt_high, kt_low = sem("kt_high"), sem("kt_low")
        k_full, k_high, k_low = sem("k_full"), sem("k_high"), sem("k_low")
        v_full, vT_ok, vt_full = sem("v_full"), sem("vT_ok"), sem("vt_full")
        v_high, v_res, v_mid, v_parts = sem("v_high"), sem("v_res"), sem("v_mid"), sem("v_parts")
        qrow_ok, qbd_ok, q_high, q_low = sem("qrow_ok"), sem("qbd_ok"), sem("q_high"), sem("q_low")
        s_full, sadd, p_high, p_low = sem("s_full"), sem("sadd"), sem("p_high"), sem("p_low")
        pv_full, pv_read, norm, o_sum = sem("pv_full"), sem("pv_read"), sem("norm"), sem("o_sum")
        probs, pads, inv_ok = sem("probs"), sem("pads"), sem("inv_ok")

        PRIMED = (s_full, pv_full, p_high, p_low, row_free, vt_full, v_res, v_parts, q_low, pv_read, qrow_ok)

        def after(eng, s, n):
            eng.wait_ge(s, n + 1 if s in PRIMED else n)

        def row_uses(l, last):
            names = [(n, 0) for n in ("logit", "ti", "pT", "semq", "semk")] if l else []
            for g in range(G):
                names += [(n, g) for n in ("max0", "max1", "max2", "max3", "shift")]
                if g:
                    names.append(("oT", g - 1))
                if g == G - 2 and not (l and last):
                    names.append(("cmax", g))
            return names + ([] if last else [("kt", 0)]) + [("oT", G - 1)]

        USES = [1 + (B - 1) * len(row_uses(l, False)) + len(row_uses(l, True)) for l in range(LAYERS)]

        def is_last(i):
            return isinstance(i, int) and i == B - 1

        def row_use(l, i, name, g=0):
            if name == "kt" and isinstance(i, int):
                return sum(USES[:l])
            return i * len(row_uses(l, False)) + (sum(USES[:l]) + 1 + row_uses(l, is_last(i)).index((name, g)))

        def step(l, i, g):
            return i * G + (l * STEPS + g)

        block = stack.enter_context(nc.Block())

        @block.sync
        def _(sp):
            sp.dma_start(const[:], const_d[:, 0:P + 3 * HG]).then_inc(const_in, 16)
            sp.dma_start(sel_raw, const_d[:, P + 3 * HG:]).then_inc(const_in, 16)
            sp.dma_start(bias[:], bias_d).then_inc(const_in, 16)
            sp.dma_start(mask[:], mask_d).then_inc(const_in, 16)
            sp.dma_start(raw[:], ctx_d[0]).then_inc(ctx_in, 16)

            def linear_half(l, half, first):
                sp.dma_start(xh, (x1_d if l == LAYERS else x_d)[half]).then_inc(xh_in, 16)

            for l in range(LAYERS):
                sp.wait_ge(ctx_low, KT * (l * B + 1))
                sp.dma_start(wq, wq_d[l]).then_inc(wq_in, 16)
                for half in range(2):
                    if half:
                        sp.wait_ge(q_evac, CT * (2 * l + 1))
                        if l:
                            sp.wait_ge(x1_out, 16)
                    sp.dma_start(xh, x_d[half]).then_inc(xh_in, 16)
                    if l == 1:
                        if half == 0:
                            after(sp, pv_full, STEPS)
                            sp.dma_start(wo, wo_d[0]).then_inc(wo_in, 16)
                        sp.wait_ge(out_evac, CT * (half + 1))
                        sp.dma_start(x1_d[half], xh).then_inc(x1_out, 16)
                sp.wait_ge(q_evac, CT * 2 * (l + 1))
                if l:
                    sp.wait_ge(x1_out, 32)
                with sp.Fori(0, B - l) as i:
                    sp.wait_ge(ctx_low, i * KT + KT * (l * B + 1))
                    sp.dma_start(raw[:], ctx_d[bass.ds(i + 1, 1)].rearrange("o p n -> (o p) n")).then_inc(ctx_in, 16)
            sp.wait_ge(ctx_low, KT * LAYERS * B)
            sp.dma_start(xh, x1_d[0]).then_inc(xh_in, 16)
            after(sp, pv_full, LAYERS * STEPS)
            sp.dma_start(wo, wo_d[1]).then_inc(wo_in, 16)
            for half in range(2):
                if half:
                    sp.wait_ge(y_out, 16)
                    sp.dma_start(xh, x1_d[1]).then_inc(xh_in, 16)
                sp.wait_ge(out_evac, CT * (half + 3))
                sp.dma_start(out_d[half], xh).then_inc(y_out, 16)
            sp.wait_ge(y_out, 32)

        @block.tensor
        def _(pe):
            lin = [0]

            def linear(weight, src, half, evac_of):
                for c in range(CT):
                    n = lin[0]
                    if c >= 2:
                        pe.wait_ge(evac_of, CT * half + c - 1)
                    for k in range(CT):
                        mm = nc.tensor.matmul(banks[n % 2][:, 0:MT], weight[:, k, c * P:(c + 1) * P], src(k),
                                              start=(k == 0), stop=(k == CT - 1))
                    mm.then_inc(lin_full, 1)
                    lin[0] += 1

            def out_phase(l):
                for half in range(2):
                    pe.wait_ge(wo_in, 16 * (l + 1))
                    pe.wait_ge(q_evac, CT * (2 * (l + 1) + (half if l == 0 else 0)))
                    if half and l == 1:
                        pe.wait_ge(out_evac, CT * 3)
                    linear(wo, lambda k: qo[:, k, half * MT:(half + 1) * MT], 2 * l + half, out_evac)
                    if l == 0:
                        q_half(1, half)

            def q_half(l, half):
                pe.wait_ge(wq_in, 16 * (l + 1))
                if l:
                    pe.wait_ge(out_evac, CT * (half + 1))
                else:
                    pe.wait_ge(xh_in, 16 * (half + 1))
                    if half:
                        pe.wait_ge(q_evac, CT)
                linear(wq, lambda k: xh[:, k, :], 2 * l + half, q_evac)

            def pairs(out, hi_lo_w, hi_lo_x, n_k, each_k=None):
                for k in range(n_k):
                    if each_k:
                        each_k(k)
                    for m, (a, b) in enumerate(((0, 0), (0, 1), (1, 0))):
                        mm = nc.tensor.matmul(out, hi_lo_w[a](k), hi_lo_x[b](k), start=(k == 0 and m == 0),
                                              stop=(k == n_k - 1 and m == 2))
                return mm

            def weights(w, g):
                return [lambda k, t=t: t[:, w, k, g * P:(g + 1) * P] for t in (w_hi, w_lo)]

            def tokens(a, b):
                return [lambda k, t=t: t[:, k, a:b] for t in (c_hi, c_lo)]

            def k_text(l, i):
                after(pe, row_free, row_use(l, i, "kt"))
                for g in range(G):
                    mm = pairs(rows[:, 0, g * TP:(g + 1) * TP], weights(0, g), tokens(0, TP), KT)
                mm.then_inc(row_full, 1)

            def k_unit(l, i, g, c):
                u = step(l, i, g)
                after(pe, v_res, 2 * u)
                each = (lambda k: pe.wait_ge(ctx_low, i * KT + (KT * (l * B + 1) + k + 1))) if g == G and c == 0 else None
                pairs(banks[c][:, 0:HALF], weights(1, g % G), tokens(TP + c * HALF, TP + (c + 1) * HALF),
                      KT, each).then_inc(k_full, 1)

            def v_unit(l, i, g, c):
                u = step(l, i, g)
                pe.wait_ge(k_low, 2 * u + (c + 1))
                if c == 0:
                    pairs(bankA[:, 0:TP], weights(2, g % G), tokens(0, TP), KT)
                    mm = pairs(bankA[:, TP:TP + HALF], weights(3, g % G), tokens(TP, TP + HALF), KT)
                else:
                    mm = pairs(bankB[:, 0:HALF], weights(3, g % G), tokens(TP + HALF, TOKP), KT)
                mm.then_inc(v_full, 1)

            def v_turn(l, i, g, c):
                u = step(l, i, g)
                pe.wait_ge(vT_ok, 2 * u + (c + 1))
                for n, t in enumerate(range(4) if c == 0 else range(4, NT)):
                    a = TP + (t - 1) * KEY if t else 0
                    mm = nc.tensor.transpose(banks[c][0:KEY, n * P:(n + 1) * P], vT[:, a:a + KEY], ident)
                mm.then_inc(vt_full, 1)

            def max_scores(l, i, g, h):
                t = step(l, i, g)
                if h == 0:
                    pe.wait_ge(q_high, t + 1)
                    pe.wait_ge(k_high, 2 * t + 2)
                    pe.wait_ge(kt_high, i + (l * B + 1))
                after(pe, row_free, row_use(l, i, f"max{h}", g))
                nc.tensor.matmul(rows[0:S, 0, 0:HALF], q_hi[:, h, :], k_hi[:, g % 2, 0:HALF], start=True, stop=True)
                nc.tensor.matmul(rows[0:S, 0, HALF:HALF + TP], q_hi[:, h, :], kt_hi[:, g, :], start=True, stop=True)
                nc.tensor.matmul(rows[0:S, 1, 0:HALF], q_hi[:, h, :], k_hi[:, g % 2, HALF:IPP],
                                 start=True, stop=True).then_inc(row_full, 1)

            def max_turn(l, i, g):
                after(pe, row_free, row_use(l, i, "shift", g))
                nc.tensor.transpose(rows[:, 0, 0:S], mx[:], ident[0:S, 0:S]).then_inc(row_full, 1)

            def context_turn(l, i):
                pe.wait_ge(ctx_chain, i * 6 + (6 * (l * B + 1) + 1))
                after(pe, row_free, row_use(l, i, "cmax", G - 2))
                nc.tensor.transpose(rows[:, 0, 0:P], cs[:, 0:1].to_broadcast([P, P]), ident).then_inc(row_full, 1)

            def score_tile(l, i, g, j):
                t = step(l, i, g)
                if j == 0:
                    after(pe, q_low, t + 1)
                    pe.wait_ge(k_low, 2 * t + 2)
                    pe.wait_ge(kt_low, i + (l * B + 1))
                after(pe, p_high, t * NT + max(j - 1, 0))
                n = KEY if j else TP
                out = st[0:n, j % 2, 0:Q4]
                hi = k_hi[:, g % 2, (j - 1) * KEY:j * KEY] if j else kt_hi[:, g, :]
                lo = k_lo[:, g % 2, (j - 1) * KEY:j * KEY] if j else kt_lo[:, g, :]
                nc.tensor.matmul(out, hi, q_hi[:, :, :], start=True, stop=False)
                nc.tensor.matmul(out, hi, q_lo[:, :, :], start=False, stop=False)
                nc.tensor.matmul(out, lo, q_hi[:, :, :], start=False, stop=False)
                if j == 0:
                    after(pe, row_free, row_use(l, i, "shift", g) + 1)
                nc.tensor.matmul(out, sel[:, min(j, 1), 0:n], shift[:, :, :], start=False, stop=True).then_inc(s_full, 1)

            def weigh(l, i, g, half):
                t = step(l, i, g)
                if half == 0:
                    after(pe, p_low, t * NT + NT)
                    after(pe, v_parts, 2 * t + 2)
                    after(pe, pv_read, t)
                for h in range(half * 2, half * 2 + 2):
                    for part, tiles in ((0, (0,)), (1, range(1, NT))):
                        for j in tiles:
                            n = TEXT if j == 0 else LAST if j == NT - 1 else KEY
                            for m, p in enumerate((p_hi, p_lo)):
                                mm = nc.tensor.matmul(pv[:, part, h * VS:(h + 1) * VS], p[0:n, j, h * S:h * S + P],
                                                      vst[0:n, g % 2, j, h, :], start=(j == tiles[0] and m == 0),
                                                      stop=(j == tiles[-1] and m == 1))
                if half:
                    mm.then_inc(pv_full, 1)

            def o_turn(l, i, g):
                pe.wait_ge(o_sum, step(l, i, g) + 1)
                after(pe, row_free, row_use(l, i, "oT", g))
                nc.tensor.transpose(rows[:, 0, 0:S], acc[:, 0].rearrange("s h d -> s (h d)"),
                                    ident[0:S, 0:S]).then_inc(row_full, 1)

            def project(l, i, g):
                return (lambda: k_unit(l, i, g, 0), lambda: k_unit(l, i, g, 1), lambda: v_unit(l, i, g, 0),
                        lambda: v_unit(l, i, g, 1), lambda: v_turn(l, i, g, 0), lambda: v_turn(l, i, g, 1))

            def nothing():
                return (lambda: None,) * 6

            def semantic(l, i, k0):
                after(pe, qrow_ok, i + (l * B + 1))
                after(pe, row_free, row_use(l, i, "logit"))
                for g in range(G):
                    mm = nc.tensor.matmul(rows[0:S, 0, 0:TP], q_row[:, g, :], kt32[:, g, :],
                                          start=(g == 0), stop=(g == G - 1))
                mm.then_inc(row_full, 1)
                after(pe, row_free, row_use(l, i, "ti"))
                for c in range(2):
                    mm = pairs(rows[0:TP, c, 0:HALF], tokens(0, TP), tokens(TP + c * HALF, TP + (c + 1) * HALF), KT)
                mm.then_inc(row_full, 1)
                pe.wait_ge(probs, i * 5 + 5)
                after(pe, row_free, row_use(l, i, "pT"))
                nc.tensor.transpose(rows[:, 0, 0:S], mx[:], ident[0:S, 0:S]).then_inc(row_full, 1)
                after(pe, row_free, row_use(l, i, "semq"))
                for c in range(2):
                    mm = nc.tensor.matmul(rows[0:S, c, 0:HALF], pT[:], ti[0:TEXT, c, :], start=True, stop=True)
                mm.then_inc(row_full, 1)
                k0()
                after(pe, row_free, row_use(l, i, "semk"))
                tif = ti[0:TEXT].rearrange("p c t -> p (c t)")
                for j in range(NIP):
                    mm = nc.tensor.matmul(rows[0:KEY, j // 3, j % 3 * S:(j % 3 + 1) * S],
                                          tif[:, j * KEY:(j + 1) * KEY], pT[:], start=True, stop=True)
                mm.then_inc(row_full, 1)

            def row(l, i):
                for g in range(G):
                    new_row = g == G - 1 and not is_last(i)
                    units = project(l, i, g + 1) if g < G - 1 or new_row else nothing()
                    k0, k1, v0, v1, t0, t1 = nothing() if g == G - 1 else units
                    if l and g == 0:
                        semantic(l, i, k0)
                    else:
                        k0()
                    max_scores(l, i, g, 0)
                    if g:
                        weigh(l, i, g - 1, 0)
                    max_scores(l, i, g, 1)
                    if g:
                        weigh(l, i, g - 1, 1)
                    max_scores(l, i, g, 2)
                    k1()
                    max_scores(l, i, g, 3)
                    v0()
                    max_turn(l, i, g)
                    score_tile(l, i, g, 0)
                    if g:
                        o_turn(l, i, g - 1)
                    score_tile(l, i, g, 1)
                    if g == G - 2 and not (l and is_last(i)):
                        context_turn(l, i)
                    v1()
                    score_tile(l, i, g, 2)
                    score_tile(l, i, g, 3)
                    t0()
                    if new_row:
                        units[0]()
                    score_tile(l, i, g, 4)
                    score_tile(l, i, g, 5)
                    t1()
                    if new_row:
                        units[1]()
                    score_tile(l, i, g, 6)
                if new_row:
                    k_text(l, i)
                weigh(l, i, G - 1, 0), weigh(l, i, G - 1, 1)
                for unit in (units[2:4] if new_row else ()):
                    unit()
                o_turn(l, i, G - 1)
                for unit in (units[4:] if new_row else ()):
                    unit()

            pe.wait_ge(const_in, 64)
            for half in range(2):
                q_half(0, half)
            for l in range(LAYERS):
                pe.wait_ge(w_low, 8 * (l + 1))
                pe.wait_ge(q_evac, 2 * CT * (l + 1))
                pe.wait_ge(sel_ok, 2)
                pe.wait_ge(pads, l + 1)
                first = project(l, -1, G)
                first[0](), first[1]()
                k_text(l, -1)
                for unit in first[2:]:
                    unit()
                with pe.Fori(0, B - 1) as i:
                    row(l, i)
                row(l, B - 1)
                after(pe, row_free, row_use(l, B - 1, "oT", G - 1) + 1)
                out_phase(l)

        @block.scalar
        def _(act):
            def load_weight(l, w):
                if w or l:
                    act.wait_ge(w_low, 2 * (4 * l + w))
                if l and w == 0:
                    after(act, pv_full, l * STEPS)
                act.dma_start(w_raw, w_d[l * 4 + w]).then_inc(w_in, 16)

            def split_weight(l, w):
                act.wait_ge(w_chain, 6 * (4 * l + w) + 6)
                for n in range(2):
                    a, b = n * KT // 2, (n + 1) * KT // 2
                    nc.scalar.activation(w_hi[:, w, a:b, :].rearrange("p k c -> p (k c)"), w_raw[:, a * C:b * C],
                                         ACT.Copy, scale=wscale[:, w:w + 1]).then_inc(w_high, 1)

            def split_context(k):
                nc.scalar.activation(c_hi[:, k, :], ctx_raw[:, k, :], ACT.Copy, scale=cs[:, 4:5]).then_inc(ctx_high, 1)

            def q_half(l, half):
                for c in range(CT):
                    n = (CT * half + c) if l == 0 else 2 * CT + 2 * CT * half + CT + c
                    act.wait_ge(lin_full, n + 1)
                    nc.scalar.activation(qo[:, c, half * MT:(half + 1) * MT], banks[n % 2][:, 0:MT],
                                         ACT.Copy).then_inc(q_evac, 1)

            def k_text(l, i):
                act.wait_ge(row_full, row_use(l, i, "kt") + 1)
                after(act, s_full, i * G * NT + (l * STEPS + G) * NT)
                nc.scalar.activation(kt32[:].rearrange("p g t -> p (g t)"), rows[:, 0, 0:G * TP], ACT.Copy,
                                     scale=inv[:, 0:1]).then_inc(row_free, 1)
                after(act, row_free, row_use(l, i, "kt") + 1)
                nc.scalar.activation(kt_hi[:], kt32[:], ACT.Copy).then_inc(kt_high, 1)

            def k_unit(l, i, g, c):
                u = step(l, i, g)
                act.wait_ge(k_full, 2 * u + (c + 1))
                if g == G and c == 0:
                    act.wait_ge(inv_ok, i + (l * B + 2))
                after(act, s_full, (u if g == G else u - 1) * NT)
                nc.scalar.activation(k_hi[:, g % G % 2, c * HALF:(c + 1) * HALF], banks[c][:, 0:HALF], ACT.Copy,
                                     scale=inv[:, 1:2]).then_inc(k_high, 1)

            def v_unit(l, i, g, c):
                u = step(l, i, g)
                act.wait_ge(v_full, 2 * u + (c + 1))
                after(act, vt_full, 2 * u)
                if c == 0:
                    nc.scalar.activation(vT[:, 0:TP], bankA[:, 0:TP], ACT.Copy, scale=inv[:, 2:3])
                    last = nc.scalar.activation(vT[:, TP:TP + HALF], bankA[:, TP:TP + HALF], ACT.Copy, scale=inv[:, 3:4])
                else:
                    last = nc.scalar.activation(vT[:, TP + HALF:TOKP], bankB[:, 0:HALF], ACT.Copy, scale=inv[:, 3:4])
                last.then_inc(vT_ok, 1)

            def v_turn(l, i, g, c):
                u = step(l, i, g)
                after(act, vt_full, 2 * u + (c + 1))
                after(act, pv_full, u if g == G else u - 1)
                a, b = (0, 4) if c == 0 else (4, NT)
                nc.scalar.activation(vst[0:KEY, g % G % 2, a:b, :, 0:D].rearrange("p t h d -> p (t h) d"),
                                     banks[c][0:KEY, 0:(b - a) * P].rearrange("p (n d) -> p n d", d=D),
                                     ACT.Copy).then_inc(v_high, 1)

            def q_high_part(l, i, g):
                t = step(l, i, g)
                act.wait_ge(qbd_ok, t + 1)
                after(act, s_full, t * NT)
                nc.scalar.activation(q_hi[:], qbd[:], ACT.Copy).then_inc(q_high, 1)

            def exps(l, i, g, j):
                t = step(l, i, g)
                if l and j:
                    act.wait_ge(sadd, (t - STEPS) * NIP + j)
                    src = prob[0:KEY, j % 3, :]
                else:
                    after(act, s_full, t * NT + (j + 1))
                    src = st[0:KEY if j else TP, j % 2, 0:Q4]
                if j == 0:
                    after(act, pv_full, t)
                after(act, p_low, t * NT + (j - 2 if j >= 3 else 0))
                n = KEY if j else TP
                nc.scalar.activation(p_hi[0:n, j, 0:Q4], src, ACT.Exp, scale=SC)
                nc.scalar.activation(prob[0:n, j % 3, :], src, ACT.Exp, scale=SC).then_inc(p_high, 1)

            def o_turn(l, i, g):
                act.wait_ge(row_full, row_use(l, i, "oT", g) + 1)
                nc.scalar.activation(qo[:, g, bass.ds(i * S, S)], rows[:, 0, 0:S], ACT.Copy).then_inc(row_free, 1)

            def project(l, i, g):
                return (lambda: k_unit(l, i, g, 0), lambda: k_unit(l, i, g, 1), lambda: v_unit(l, i, g, 0),
                        lambda: v_unit(l, i, g, 1), lambda: v_turn(l, i, g, 0), lambda: v_turn(l, i, g, 1))

            def nothing():
                return (lambda: None,) * 6

            def new_units(l, i):
                k0, k1, v0, v1, t0, t1 = project(l, i, G)
                k0(), k1()
                k_text(l, i)
                v0(), v1()
                if not isinstance(i, int):
                    o_turn(l, i, G - 1)
                t0(), t1()

            def row(l, i):
                if l:
                    act.wait_ge(row_full, row_use(l, i, "logit") + 1)
                    act.wait_ge(probs, i * 5 + 2)
                    nc.scalar.activation(mx[:, 0:TEXT], rows[0:S, 0, 0:TEXT], ACT.Exp, bias=sm[:, 1:2],
                                         scale=SC).then_inc(row_free, 1)
                for g in range(G):
                    k0, k1, v0, v1, t0, t1 = project(l, i, g + 1) if g < G - 1 else nothing()
                    new_context = g == G - 1 and not (l and is_last(i))
                    q_high_part(l, i, g)
                    k0()
                    if new_context:
                        act.wait_ge(ctx_chain, i * 6 + 6 * (l * B + 2))
                        for k in range(KT):
                            split_context(k)
                    k1()
                    v0()
                    exps(l, i, g, 0)
                    if g:
                        o_turn(l, i, g - 1)
                    exps(l, i, g, 1)
                    v1()
                    exps(l, i, g, 2)
                    exps(l, i, g, 3)
                    t0()
                    exps(l, i, g, 4)
                    exps(l, i, g, 5)
                    t1()
                    exps(l, i, g, 6)
                if is_last(i):
                    o_turn(l, i, G - 1)
                else:
                    new_units(l, i)

            load_weight(0, 0)
            act.wait_ge(ctx_chain, 6)
            for k in range(KT):
                split_context(k)
            for w in range(4):
                split_weight(0, w)
                if w < 3:
                    load_weight(0, w + 1)
                if w == 0:
                    q_half(0, 0)
                if w == 1:
                    q_half(0, 1)
            for l in range(LAYERS):
                new_units(l, -1)
                with act.Fori(0, B - 1) as i:
                    row(l, i)
                row(l, B - 1)
                if l == 0:
                    load_weight(1, 0)
                    q_half(1, 0)
                    split_weight(1, 0)
                    load_weight(1, 1)
                    split_weight(1, 1)
                    load_weight(1, 2)
                    q_half(1, 1)
                    split_weight(1, 2)
                    load_weight(1, 3)
                    split_weight(1, 3)

        @block.gpsimd
        def _(pool):
            def all_max(ap, chain, n):
                pool.wait_ge(chain, n)
                nc.gpsimd.partition_all_reduce(ap[:, 1:2], ap[:, 0:1], P, RMAX).then_inc(chain, 1)

            def ones_and_pads(l):
                for b in range(2):
                    nc.gpsimd.memset(vst[:, b, :, :, 3 * D:VS].rearrange("p t h v -> p (t h) v"), 1.0)
                for p in (p_hi, p_lo):
                    last = nc.gpsimd.memset(p[:, :, Q4:PW], 0.0)
                last.then_inc(pads, 1)

            def q_spread(l, i, g):
                t = step(l, i, g)
                after(pool, q_low, t)
                if g == G:
                    if l and not isinstance(i, int):
                        pool.wait_ge(row_full, row_use(l, i, "logit") + 1)
                    nc.gpsimd.tensor_copy(q_row[:], qo[:, :, bass.ds(i * S + S, S)]).then_inc(qrow_ok, 1)
                    after(pool, qrow_ok, i + (l * B + 2))
                nc.gpsimd.tensor_tensor(qbd[:], q_row[:, g % G, :].unsqueeze(1).to_broadcast([P, HG, S]),
                                        hmask.unsqueeze(2).to_broadcast([P, HG, S]), ALU.mult).then_inc(qbd_ok, 1)

            def v_turn(l, i, g, c):
                u = step(l, i, g)
                after(pool, v_res, 2 * u + (c + 1))
                a, b = (0, 4) if c == 0 else (4, NT)
                n = (b - a) * HG
                rest = v_rest[0:KEY, 0:n * D].rearrange("p (n d) -> p n d", d=D)
                one = ones[0:KEY, 0:1].unsqueeze(2).to_broadcast([KEY, n, D])
                mid, low = (vst[0:KEY, g % G % 2, a:b, :, m * D:(m + 1) * D].rearrange("p t h d -> p (t h) d")
                            for m in (1, 2))
                nc.gpsimd.tensor_tensor(mid, rest, one, ALU.mult).then_inc(v_mid, 1)
                pool.wait_ge(v_mid, 2 * u + (c + 1))
                nc.gpsimd.tensor_tensor(low, rest, mid, ALU.subtract).then_inc(v_parts, 1)

            def new_units(l, i):
                q_spread(l, i, G)
                v_turn(l, i, G, 0), v_turn(l, i, G, 1)

            def row(l, i):
                for g in range(1, G):
                    q_spread(l, i, g)
                    v_turn(l, i, g, 0), v_turn(l, i, g, 1)
                if not is_last(i):
                    new_units(l, i)

            for n, s in enumerate(PRIMED):
                nc.gpsimd.memset(primer[:, n:n + 1], 0.0).then_inc(s, 1)
            all_max(cs, ctx_chain, 1)
            for l in range(LAYERS):
                for w in range(4):
                    all_max(ws, w_chain, 6 * (4 * l + w) + 1)
                pool.wait_ge(w_low, 8 * (l + 1))
                pool.wait_ge(sel_ok, 2)
                if l:
                    pool.wait_ge(out_evac, 2 * CT)
                ones_and_pads(l)
                pool.wait_ge(q_evac, 2 * CT * (l + 1))
                new_units(l, -1)
                with pool.Fori(0, B - 1) as i:
                    row(l, i)
                row(l, B - 1)

        @block.vector
        def _(dve):
            def scale_chain(ap, chain, base, s_out, inv_out):
                dve.wait_ge(chain, base + 2)
                nc.vector.tensor_scalar(ap[:, 2:3], ap[:, 1:2], TINY, None, ALU.max).then_inc(chain, 1)
                dve.wait_ge(chain, base + 3)
                nc.vector.tensor_scalar(ap[:, 3:4].bitcast(I32), ap[:, 2:3].bitcast(I32), EXP_BITS, None,
                                        ALU.bitwise_and).then_inc(chain, 1)
                dve.wait_ge(chain, base + 4)
                nc.vector.tensor_scalar(inv_out, ap[:, 3:4], 1.0 / TOP, None, ALU.mult).then_inc(chain, 1)
                dve.wait_ge(chain, base + 5)
                nc.vector.reciprocal(s_out, inv_out).then_inc(chain, 1)

            def weight(l, w):
                n = 4 * l + w
                dve.wait_ge(w_in, 16 * (n + 1))
                nc.vector.tensor_reduce(ws[:, 0:1], w_raw, AX.X, ALU.max, apply_absolute_value=True).then_inc(w_chain, 1)
                scale_chain(ws, w_chain, 6 * n, wscale[:, w:w + 1], winv[:, w:w + 1])
                for m in range(2):
                    a, b = m * KT // 2, (m + 1) * KT // 2
                    dve.wait_ge(w_high, 2 * n + m + 1)
                    nc.vector.scalar_tensor_tensor(w_lo[:, w, a:b, :].rearrange("p k c -> p (k c)"), w_raw[:, a * C:b * C],
                                                   wscale[:, w:w + 1], w_hi[:, w, a:b, :].rearrange("p k c -> p (k c)"),
                                                   ALU.mult, ALU.subtract).then_inc(w_low, 1)

            def context_part(n, k):
                if k == 0:
                    dve.wait_ge(ctx_in, n * 16 + 16)
                nc.vector.tensor_reduce(cparts[:, k:k + 1], ctx_raw[:, k, :], AX.X, ALU.max,
                                        apply_absolute_value=True).then_inc(ctx_parts, 1)

            def context_max(n):
                dve.wait_ge(ctx_parts, n * KT + KT)
                nc.vector.tensor_reduce(cs[:, 0:1], cparts[:], AX.X, ALU.max).then_inc(ctx_chain, 1)

            def context_turn(l, i):
                dve.wait_ge(row_full, row_use(l, i, "cmax", G - 2) + 1)
                nc.vector.tensor_reduce(cs[:, 1:2], rows[:, 0, 0:P], AX.X, ALU.max).then_inc(ctx_chain, 1)
                dve.wait_ge(ctx_chain, i * 6 + (6 * (l * B + 1) + 2))
                nc.vector.tensor_copy(cs[:, 6:7], cs[:, 1:2]).then_inc(row_free, 1)

            def context_scale(n):
                scale_chain(cs, ctx_chain, n * 6, cs[:, 4:5], cs[:, 5:6])

            def split_context(n, k):
                dve.wait_ge(ctx_high, n * KT + (k + 1))
                nc.vector.scalar_tensor_tensor(c_lo[:, k, :], ctx_raw[:, k, :], cs[:, 4:5], c_hi[:, k, :],
                                               ALU.mult, ALU.subtract).then_inc(ctx_low, 1)

            def out_half(l, half):
                dve.wait_ge(xh_in, 16 * (2 * (l + 1) + half + 1))
                for c in range(CT):
                    n = 2 * CT + (2 * CT * half if l == 0 else 4 * CT + CT * half) + c
                    dve.wait_ge(lin_full, n + 1)
                    nc.vector.scalar_tensor_tensor(xh[:, c, :], banks[n % 2][:, 0:MT], bias[:, l, c:c + 1], xh[:, c, :],
                                                   ALU.add, ALU.add).then_inc(out_evac, 1)

            def k_text(l, i):
                dve.wait_ge(kt_high, i + (l * B + 2))
                nc.vector.tensor_tensor(kt_lo[:], kt32[:], kt_hi[:].bitcast(F32), ALU.subtract).then_inc(kt_low, 1)

            def k_unit(l, i, g, c):
                u = step(l, i, g)
                dve.wait_ge(k_high, 2 * u + (c + 1))
                a, b = c * HALF, (c + 1) * HALF
                nc.vector.scalar_tensor_tensor(k_lo[:, g % G % 2, a:b], banks[c][:, 0:HALF], inv[:, 1:2],
                                               k_hi[:, g % G % 2, a:b].bitcast(F32), ALU.mult, ALU.subtract).then_inc(k_low, 1)

            def v_turn(l, i, g, c):
                u = step(l, i, g)
                dve.wait_ge(v_high, 2 * u + (c + 1))
                after(dve, v_parts, 2 * u + c)
                a, b = (0, 4) if c == 0 else (4, NT)
                n = b - a
                nc.vector.tensor_tensor(v_rest[0:KEY, 0:n * P].rearrange("p (n d) -> p n d", d=D),
                                        banks[c][0:KEY, 0:n * P].rearrange("p (n d) -> p n d", d=D),
                                        vst[0:KEY, g % G % 2, a:b, :, 0:D].rearrange("p t h d -> p (t h) d"),
                                        ALU.subtract).then_inc(v_res, 1)

            def q_low_part(l, i, g):
                dve.wait_ge(q_high, step(l, i, g) + 1)
                nc.vector.tensor_tensor(q_lo[:], qbd[:], q_hi[:].bitcast(F32), ALU.subtract).then_inc(q_low, 1)

            def maxima(l, i, g, h):
                dve.wait_ge(row_full, row_use(l, i, f"max{h}", g) + 1)
                nc.vector.tensor_reduce(mx[:, h:h + 1], rows[0:S, 0, HALF:HALF + TP], AX.X, ALU.max)
                if l:
                    last = nc.vector.tensor_tensor_reduce(out=ti[0:S], in0=rows[0:S, :, 0:HALF], in1=semq[:], scale=1.0,
                                                          scalar=LOWEST, op0=ALU.add, op1=ALU.max,
                                                          accum_out=mx[:, HG + h:HG + h + 1])
                else:
                    last = nc.vector.tensor_reduce(mx[:, HG + h:HG + h + 1], rows[0:S, :, 0:HALF], AX.XY, ALU.max)
                last.then_inc(row_free, 1)

            def shift_build(l, i, g):
                dve.wait_ge(row_full, row_use(l, i, "shift", g) + 1)
                after(dve, s_full, step(l, i, g) * NT)
                nc.vector.tensor_tensor(shift[:], rows[:, 0, 0:S].unsqueeze(1).to_broadcast([P, HG, S]),
                                        nmask.unsqueeze(2).to_broadcast([P, HG, S]), ALU.mult).then_inc(row_free, 1)

            def add_semantic(l, i, g, j):
                t = step(l, i, g)
                after(dve, s_full, t * NT + (j + 1))
                after(dve, p_low, t * NT + (j - 2 if j >= 3 else 0))
                nc.vector.tensor_tensor(prob[0:KEY, j % 3, :].rearrange("p (h q) -> p h q", h=HG),
                                        st[0:KEY, j % 2, 0:Q4].rearrange("p (h q) -> p h q", h=HG),
                                        semk[:, j - 1, :].unsqueeze(1).to_broadcast([KEY, HG, S]),
                                        ALU.add).then_inc(sadd, 1)

            def prob_low(l, i, g, j):
                t = step(l, i, g)
                after(dve, p_high, t * NT + (j + 1))
                n = KEY if j else TP
                nc.vector.tensor_tensor(p_lo[0:n, j, 0:Q4], prob[0:n, j % 3, :], p_hi[0:n, j, 0:Q4],
                                        ALU.subtract).then_inc(p_low, 1)

            def normalise(l, i, g):
                t = step(l, i, g)
                after(dve, pv_full, t + 1)
                out = pv[0:S, :, 0:HG * VS].rearrange("s b (h v) -> s b h v", h=HG)
                nc.vector.reciprocal(den[:], out[:, :, :, 3 * D]).then_inc(norm, 1)
                for b in range(2):
                    nc.vector.tensor_reduce(acc[:, b], out[:, b, :, 0:3 * D].rearrange("s h (m d) -> s h d m", m=3),
                                            AX.X, ALU.add).then_inc(pv_read if b else norm, 1)
                dve.wait_ge(norm, t * 4 + 1)
                nc.vector.tensor_scalar(den[:, 1, :], den[:, 1, :], mask[:, l:l + 1], None, ALU.mult).then_inc(norm, 1)
                dve.wait_ge(norm, t * 4 + 3)
                after(dve, pv_read, t + 1)
                nc.vector.tensor_tensor(acc[:], acc[:], den[:].unsqueeze(3).to_broadcast([S, 2, HG, D]),
                                        ALU.mult).then_inc(norm, 1)
                dve.wait_ge(norm, t * 4 + 4)
                nc.vector.tensor_tensor(acc[:, 0], acc[:, 0], acc[:, 1], ALU.add).then_inc(o_sum, 1)

            def project(l, i, g):
                return (lambda: k_unit(l, i, g, 0), lambda: k_unit(l, i, g, 1), lambda: v_turn(l, i, g, 0),
                        lambda: v_turn(l, i, g, 1))

            def new_scale(l, i):
                if l or not isinstance(i, int):
                    dve.wait_ge(vT_ok, 2 * step(l, i, G))
                dve.wait_ge(ctx_chain, i * 6 + 6 * (l * B + 2))
                nc.vector.tensor_scalar(inv[:], winv[:], cs[:, 5:6], None, ALU.mult).then_inc(inv_ok, 1)

            def new_units(l, i):
                k0, k1, t0, t1 = project(l, i, G)
                k0(), k1()
                k_text(l, i)
                if not isinstance(i, int):
                    normalise(l, i, G - 1)
                t0(), t1()

            def semantic(l, i):
                dve.wait_ge(row_full, row_use(l, i, "logit") + 1)
                nc.vector.tensor_reduce(sm[:, 0:1], rows[0:S, 0, 0:TEXT], AX.X, ALU.max).then_inc(probs, 1)
                dve.wait_ge(probs, i * 5 + 1)
                nc.vector.tensor_scalar(sm[:, 1:2], sm[:, 0:1], -SC, None, ALU.mult).then_inc(probs, 1)
                q_low_part(l, i, 0)
                after(dve, row_free, row_use(l, i, "logit") + 1)
                nc.vector.tensor_reduce(sm[:, 2:3], mx[:, 0:TEXT], AX.X, ALU.add).then_inc(probs, 1)
                dve.wait_ge(probs, i * 5 + 3)
                nc.vector.reciprocal(sm[:, 3:4], sm[:, 2:3]).then_inc(probs, 1)
                dve.wait_ge(probs, i * 5 + 4)
                nc.vector.tensor_scalar(mx[:, 0:TEXT], mx[:, 0:TEXT], sm[:, 3:4], None, ALU.mult).then_inc(probs, 1)
                dve.wait_ge(row_full, row_use(l, i, "ti") + 1)
                nc.vector.tensor_scalar(ti[0:TP], rows[0:TP, :, 0:HALF], cs[0:TP, 5:6], cs[0:TP, 5:6],
                                        ALU.mult, ALU.mult).then_inc(row_free, 1)
                dve.wait_ge(row_full, row_use(l, i, "pT") + 1)
                nc.vector.tensor_copy(pT[:], rows[0:TEXT, 0, 0:S]).then_inc(row_free, 1)
                dve.wait_ge(row_full, row_use(l, i, "semq") + 1)
                nc.vector.tensor_scalar(semq[:], rows[0:S, :, 0:HALF], SEM, None, ALU.mult).then_inc(row_free, 1)
                dve.wait_ge(row_full, row_use(l, i, "semk") + 1)
                nc.vector.tensor_scalar(semk[:].rearrange("p (b t) q -> p b (t q)", b=2),
                                        rows[0:KEY, :, 0:NIP // 2 * S], SEM, None, ALU.mult).then_inc(row_free, 1)

            def row(l, i):
                for g in range(G):
                    k0, k1, t0, t1 = project(l, i, g + 1) if g < G - 1 else (lambda: None,) * 4
                    new_context = not (l and is_last(i))
                    splits = iter(range(KT)) if g == G - 1 and new_context else iter(())

                    def split(count):
                        for _, k in zip(range(count), splits):
                            split_context(i + (l * B + 1), k)

                    if l and g == 0:
                        semantic(l, i)
                    else:
                        q_low_part(l, i, g)
                    k0()
                    if g == G - 1 and not is_last(i):
                        new_scale(l, i)
                    maxima(l, i, g, 0)
                    split(1)
                    maxima(l, i, g, 1)
                    split(1)
                    maxima(l, i, g, 2)
                    if g:
                        normalise(l, i, g - 1)
                    maxima(l, i, g, 3)
                    k1()
                    shift_build(l, i, g)
                    split(1)
                    for j in range(NT):
                        if l and j < NT - 1:
                            add_semantic(l, i, g, j + 1)
                        prob_low(l, i, g, j)
                        if g == G - 2 and j == 1 and new_context:
                            context_turn(l, i)
                            context_scale(i + (l * B + 1))
                        if j == 3:
                            t0()
                        if j == 5:
                            t1()
                        if j < 2:
                            split(2 + j)
                        if g == 2 and new_context:
                            context_part(i + (l * B + 1), j)
                    if g == 2 and new_context:
                        context_part(i + (l * B + 1), NT)
                        context_max(i + (l * B + 1))
                if is_last(i):
                    normalise(l, i, G - 1)
                else:
                    new_units(l, i)

            dve.wait_ge(const_in, 64)
            nc.vector.tensor_copy(sel[:].rearrange("p a k -> p (a k)"), sel_raw).then_inc(sel_ok, 1)
            nc.vector.memset(mx[:], 0.0).then_inc(sel_ok, 1)
            for k in range(KT):
                context_part(0, k)
            context_max(0)
            context_scale(0)
            for k in range(KT):
                split_context(0, k)
            for l in range(LAYERS):
                for w in range(4):
                    if l and w % 2 == 0:
                        out_half(0, w // 2)
                    weight(l, w)
                dve.wait_ge(w_chain, 24 * (l + 1))
                if l:
                    dve.wait_ge(ctx_low, KT * (B + 1))
                new_scale(l, -1)
                new_units(l, -1)
                with dve.Fori(0, B - 1) as i:
                    row(l, i)
                row(l, B - 1)
            for half in range(2):
                out_half(1, half)


def kernel(x, ctx_2048, fside_S_0, L0_xattn_Wq, L0_xattn_Wk, L0_xattn_Wv, L0_xattn_Wk_ip, L0_xattn_Wv_ip,
           L0_xattn_Wo, L0_xattn_bo, L1_xattn_Wq, L1_xattn_Wk, L1_xattn_Wv, L1_xattn_Wk_ip, L1_xattn_Wv_ip,
           L1_xattn_Wout, L1_xattn_bout):
    import concourse.bacc as bacc
    from concourse.bass_utils import run_bass_kernel_spmd

    def rows_first(w):
        w = np.asarray(w)
        return w.reshape(-1, P, w.shape[1]).transpose(1, 0, 2).reshape(P, -1)

    ctx = np.asarray(ctx_2048)
    order = list(range(TEXT)) + [TEXT - 1] + list(range(TEXT, TOK)) + [TOK - 1] * (IPP - IP)
    ctx = ctx[:, order, :].transpose(0, 2, 1).reshape(B, KT, P, TOKP).transpose(0, 2, 1, 3).reshape(B, P, KT * TOKP)
    ctx = np.concatenate([ctx, ctx[:1]])
    xs = np.asarray(x).reshape(2, MT, CT, P).transpose(0, 3, 2, 1)
    weights = [np.asarray(w).T for w in (L0_xattn_Wk, L0_xattn_Wk_ip, L0_xattn_Wv, L0_xattn_Wv_ip)]
    weights += [np.asarray(w) for w in (L1_xattn_Wk, L1_xattn_Wk_ip, L1_xattn_Wv, L1_xattn_Wv_ip)]
    const = np.zeros((P, P + 3 * HG + 2 * KEY), np.float32)
    const[:, 0:P] = np.eye(P)
    const[:, P + 2 * HG:P + 3 * HG] = 1.0
    const[0:HG, P + 3 * HG:P + 3 * HG + KEY] = 1.0
    const[HG:2 * HG, P + 3 * HG + KEY:] = 1.0
    for h in range(HG):
        const[h * D:(h + 1) * D, P + h] = 1.0
        const[[h, HG + h], P + HG + h] = -1.0
    arrays = {
        "ctx": ctx,
        "x": xs,
        "w": np.stack([rows_first(w) for w in weights]),
        "wq": np.stack([rows_first(np.asarray(L0_xattn_Wq).T), rows_first(L1_xattn_Wq)]).reshape(LAYERS, P, CT, C),
        "wo": np.stack([rows_first(np.asarray(L0_xattn_Wo).T), rows_first(L1_xattn_Wout)]).reshape(LAYERS, P, CT, C),
        "bias": np.stack([np.asarray(b).reshape(CT, P).T for b in (L0_xattn_bo, L1_xattn_bout)], axis=1),
        "mask": np.stack([np.ones(S, np.float32), np.asarray(fside_S_0)], axis=1),
        "const": const,
    }
    arrays = {f"{n}_dram": np.ascontiguousarray(a) for n, a in arrays.items()}
    nc = bacc.Bacc("TRN2", target_bir_lowering=False, num_devices=1)
    ins = [nc.dram_tensor(n, a.shape, mybir.dt.from_np(a.dtype), kind="ExternalInput").ap() for n, a in arrays.items()]
    x1 = nc.dram_tensor("x1_dram", (2, P, CT, MT), F32, kind="Internal").ap()
    out = nc.dram_tensor("out_dram", (2, P, CT, MT), F32, kind="ExternalOutput").ap()
    xattn_pair_kernel(nc, *ins, x1, out)
    got = run_bass_kernel_spmd(nc, [arrays], core_ids=[0]).results[0]["out_dram"]
    return got.transpose(0, 3, 2, 1).reshape(B, S, C)
```

```python
from contextlib import ExitStack

import concourse.bass as bass
import numpy as np
from concourse import mybir

ALU = mybir.AluOpType
ACT = mybir.ActivationFunctionType
AX = mybir.AxisListType
F32 = mybir.dt.float32
F32R = mybir.dt.float32r
F16 = mybir.dt.float16
I32 = mybir.dt.int32
RMAX = bass.bass_isa.ReduceOp.max

P = 128
B, S, C, CC = 8, 100, 640, 1024
TOK = 722
H, D = 20, 32
TEXT = 77
IP = TOK - TEXT
LAYERS = 2
HG = P // D
G = H // HG
KT = CC // P
CT = C // P
KEY = 108
NIP = -(-IP // KEY)
NT = 1 + NIP
TP = TEXT + 1
IPP = KEY * NIP
HALF = IPP // 2
LAST = IP - KEY * (NIP - 1)
TOKP = TP + IPP
Q4 = HG * S
VS = 2 * D + 2
PW = Q4 + 32
MT = B * S // 2
STEPS = B * G
QK = KT // 4
QW = QK * C
SLOTS = 6
PLACES = ((0, 1, 2, 3) * 2 + (4, 5, 0, 1, 2, 3, 4, 5), tuple((n + 4) % SLOTS for n in range(16)))
ORDER = (1, 0, 2, 3)
EARLY = 2
SC = float(D) ** -0.5
SEM = 0.5
TINY = 1e-30
VSC = 2.0 ** -25
TOP = 2.0 ** 14
EXP_BITS = 0x7F800000
LOWEST = -3.0e38


def xattn_pair_kernel(nc, ctx_d, x_d, w_d, wq_d, wo_d, bias_d, mask_d, const_d, x1_d, out_d):
    with ExitStack() as stack:
        def sb(name, shape, dt):
            return stack.enter_context(nc.sbuf_tensor(name, shape, dt))

        def psum(name, shape, dt=F32):
            return stack.enter_context(nc.psum_tensor(name, shape, dt))

        def sem(name):
            return stack.enter_context(nc.semaphore(name))

        w_hi = sb("w_hi", [P, 4, KT, C], F16)
        w_lo = sb("w_lo", [P, 4, KT, C], F16)
        c_hi = sb("c_hi", [P, KT, TOKP], F16)
        c_lo = sb("c_lo", [P, KT, TOKP], F16)
        raw = sb("raw", [P, KT * TOKP], F32)
        ctx_raw = raw[:, :].rearrange("p (k t) -> p k t", k=KT)
        qo = sb("qo", [P, CT, B * S], F32)
        work = sb("work", [P, KT * C], F32)
        slots = [work[:, n * QW:(n + 1) * QW] for n in range(4)]
        slots += [raw[:, CT * C + n * QW:CT * C + (n + 1) * QW] for n in range(2)]
        ends = np.cumsum([0, NT * HG * VS, TOKP, 3 * Q4, Q4, 2 * HG * D])
        vst, vT, prob, qbd, acc = (work[:, int(a):int(b)] for a, b in zip(ends, ends[1:]))
        vst = vst.bitcast(F16).rearrange("p (b t h v) -> p b t h v", b=2, t=NT, h=HG)
        prob = prob.rearrange("p (r q) -> p r q", r=3)
        qbd = qbd.rearrange("p (h q) -> p h q", h=HG)
        acc = acc[0:S].rearrange("s (b h d) -> s b h d", b=2, h=HG)
        pwork = sb("pwork", [P, CT * C], F32)
        wq = pwork[:, :].rearrange("p (k n) -> p k n", k=CT)
        wo = raw[:, 0:CT * C].rearrange("p (k n) -> p k n", k=CT)
        p_hi = pwork[:, 0:NT * PW // 2].bitcast(F16).rearrange("p (t q) -> p t q", t=NT)
        p_lo = pwork[:, NT * PW // 2:NT * PW].bitcast(F16).rearrange("p (t q) -> p t q", t=NT)
        k_hi = sb("k_hi", [P, 2, TOKP], F32R)
        k_lo = sb("k_lo", [P, 2, IPP], F32R)
        extra = sb("extra", [P, 2 * IPP + NIP * S + CT * S], F32)
        xh = extra[:, 0:CT * MT].rearrange("p (c t) -> p c t", c=CT)
        xr = raw[:, CT * C:CT * C + CT * MT].rearrange("p (c t) -> p c t", c=CT)
        semq = extra[0:S, 0:IPP].rearrange("p (b t) -> p b t", b=2)
        ti = extra[:, IPP:2 * IPP].rearrange("p (b t) -> p b t", b=2)
        semk = extra[0:KEY, 2 * IPP:2 * IPP + NIP * S].rearrange("p (t q) -> p t q", t=NIP)
        q_row = extra[:, 2 * IPP + NIP * S:].rearrange("p (c q) -> p c q", c=CT)
        kt32 = sb("kt32", [P, G, TP], F32)
        sel_raw = kt32[:].rearrange("p g t -> p (g t)")[:, 0:2 * KEY]
        kt_hi = sb("kt_hi", [P, G, TP], F32R)
        kt_lo = sb("kt_lo", [P, G, TP], F32R)
        q_hi = sb("q_hi", [P, 2, HG, S], F32R)
        q_lo = sb("q_lo", [P, HG, S], F32R)
        shift = sb("shift", [P, HG, S], F32R)
        sel = sb("sel", [P, 2, KEY], F32R)
        const = sb("const", [P, P + 2 * HG], F32)
        ident = const[:, 0:P]
        hmask = const[:, P:P + HG]
        nmask = const[:, P + HG:P + 2 * HG]
        bias = sb("bias", [P, LAYERS, CT], F32)
        mask = sb("mask", [S, LAYERS], F32)
        mx = sb("mx", [S, P], F32)
        pT = sb("pT", [TEXT, S], F32)
        den = sb("den", [S, 2, HG], F32)
        back = sb("back", [S, 2], F32)
        wscale = sb("wscale", [P, 4], F32)
        wparts = sb("wparts", [P, 2, 4], F32)
        winv = sb("winv", [P, 4], F32)
        cs = sb("cs", [P, 8], F32)
        cparts = sb("cparts", [P, KT], F32)
        ws = sb("ws", [P, 4], F32)
        inv = sb("inv", [P, 4], F32)
        sm = sb("sm", [S, 4], F32)
        primer = sb("primer", [1, 16], F32)

        proj = psum("proj", [P, 2, 512])
        bankA, bankB = proj[:, 0, :], proj[:, 1, :]
        rows = psum("rows", [P, 2, 512])
        st = psum("st", [P, 2, 512])
        pv = psum("pv", [P, 2, 512])
        banks = (bankA, bankB)

        const_in, sel_ok = sem("const_in"), sem("sel_ok")
        w_parts = sem("w_parts")
        w_in = [sem(f"w_in{n}") for n in range(SLOTS)]
        w_chain, w_high, w_low = sem("w_chain"), sem("w_high"), sem("w_low")
        ctx_parts = sem("ctx_parts")
        ctx_in, ctx_chain, ctx_high = sem("ctx_in"), sem("ctx_chain"), sem("ctx_high")
        ctx_scaled = sem("ctx_scaled")
        ctx_low = (sem("ctx_low_even"), sem("ctx_low_odd"))
        wq_in, wo_in, xh_in = sem("wq_in"), sem("wo_in"), sem("xh_in")
        x1_out, y_out = sem("x1_out"), sem("y_out")
        lin_full, q_evac, out_evac = sem("lin_full"), sem("q_evac"), sem("out_evac")
        row_full, row_free = sem("row_full"), sem("row_free")
        kt_high, kt_low = sem("kt_high"), sem("kt_low")
        k_full, k_high, k_low = sem("k_full"), sem("k_high"), sem("k_low")
        v_full, vT_ok, vt_full = sem("v_full"), sem("vT_ok"), sem("vt_full")
        v_high, v_low, back_ok = sem("v_high"), sem("v_low"), sem("back_ok")
        qrow_ok, qbd_ok, q_high, q_low = sem("qrow_ok"), sem("qbd_ok"), sem("q_high"), sem("q_low")
        s_full, sadd, p_high, p_low = sem("s_full"), sem("sadd"), sem("p_high"), sem("p_low")
        pv_full, pv_read, norm, o_sum = sem("pv_full"), sem("pv_read"), sem("norm"), sem("o_sum")
        probs, pads, inv_ok = sem("probs"), sem("pads"), sem("inv_ok")

        PRIMED = (s_full, pv_full, p_high, p_low, row_free, vt_full, v_low, q_low, pv_read, qrow_ok)

        def after(eng, s, n):
            eng.wait_ge(s, n + 1 if s in PRIMED else n)

        def split_contexts(eng, n):
            for s in ctx_low:
                eng.wait_ge(s, n * KT // 2)

        def row_uses(l, last):
            names = [(n, 0) for n in ("logit", "ti", "pT", "semq", "semk")] if l else []
            for g in range(G):
                names += [(n, g) for n in ("max0", "max1", "max2", "max3", "shift")]
                if 0 < g < G - 1:
                    names.append(("oT", g - 1))
                if g == G - 3 and not (l and last):
                    names.append(("cmax", g))
            return names + ([] if last else [("kt", 0)]) + [("oT", G - 2), ("oT", G - 1)]

        USES = [1 + (B - 1) * len(row_uses(l, False)) + len(row_uses(l, True)) for l in range(LAYERS)]

        def is_last(i):
            return isinstance(i, int) and i == B - 1

        def row_use(l, i, name, g=0):
            if name == "kt" and isinstance(i, int):
                return sum(USES[:l])
            return i * len(row_uses(l, False)) + (sum(USES[:l]) + 1 + row_uses(l, is_last(i)).index((name, g)))

        def slot(l, n):
            return PLACES[l][n]

        def before(l, n):
            return max((m for m in range(n) if slot(l, m) == slot(l, n)), default=None)

        def arrived(l, n):
            return 16 * sum(slot(a, b) == slot(l, n) for a in range(l + 1) for b in range(16 if a < l else n + 1))

        def step(l, i, g):
            return i * G + (l * STEPS + g)

        block = stack.enter_context(nc.Block())

        @block.sync
        def _(sp):
            sp.dma_start(const[:], const_d[:, 0:P + 2 * HG]).then_inc(const_in, 16)
            sp.dma_start(sel_raw, const_d[:, P + 2 * HG:]).then_inc(const_in, 16)
            sp.dma_start(bias[:], bias_d).then_inc(const_in, 16)
            sp.dma_start(mask[:], mask_d).then_inc(const_in, 16)
            sp.dma_start(raw[:], ctx_d[0]).then_inc(ctx_in, 16)
            for l in range(LAYERS):
                if l:
                    split_contexts(sp, B + 1)
                    sp.dma_start(wo, wo_d[0]).then_inc(wo_in, 16)
                else:
                    sp.dma_start(wq, wq_d[0]).then_inc(wq_in, 16)
                for half in range(2):
                    if half:
                        sp.wait_ge(q_evac, CT * (2 * l + 1))
                        if l:
                            sp.wait_ge(x1_out, 16)
                    elif l:
                        after(sp, s_full, STEPS * NT)
                    sp.dma_start(xh, x_d[half]).then_inc(xh_in, 16)
                    if l == 1:
                        if half == 0:
                            after(sp, pv_full, STEPS)
                            sp.dma_start(wq, wq_d[1]).then_inc(wq_in, 16)
                        sp.wait_ge(out_evac, CT * (half + 1))
                        sp.dma_start(x1_d[half], xh).then_inc(x1_out, 16)
                sp.wait_ge(q_evac, CT * 2 * (l + 1))
                sp.wait_ge(w_low, 16 * (l + 1))
                with sp.Fori(0, B - l) as i:
                    for s in ctx_low:
                        sp.wait_ge(s, i * (KT // 2) + KT // 2 * (l * B + 1))
                    sp.dma_start(raw[:], ctx_d[bass.ds(i + 1, 1)].rearrange("o p n -> (o p) n")).then_inc(ctx_in, 16)
            split_contexts(sp, LAYERS * B)
            sp.dma_start(wo, wo_d[1]).then_inc(wo_in, 16)
            sp.dma_start(xr, x1_d[0]).then_inc(xh_in, 16)
            sp.wait_ge(xh_in, 16 * 5)
            after(sp, pv_full, LAYERS * STEPS)
            sp.dma_start(xh, x1_d[1]).then_inc(xh_in, 16)
            sp.wait_ge(out_evac, CT * 3)
            sp.dma_start(out_d[0], xr).then_inc(y_out, 16)
            for c in range(CT):
                sp.wait_ge(out_evac, CT * 3 + c + 1)
                sp.dma_start(out_d[1][:, c], xh[:, c, :]).then_inc(y_out, 16)
            sp.wait_ge(y_out, 16 * (CT + 1))

        @block.tensor
        def _(pe):
            lin = [0]

            def linear(weight, src, half, evac_of, tiles=range(CT)):
                for c in tiles:
                    n = lin[0]
                    if c >= 2:
                        pe.wait_ge(evac_of, CT * half + c - 1)
                    for k in range(CT):
                        mm = nc.tensor.matmul(banks[n % 2][:, 0:MT], weight[:, k, c * P:(c + 1) * P], src(k),
                                              start=(k == 0), stop=(k == CT - 1))
                    mm.then_inc(lin_full, 1)
                    lin[0] += 1

            def out_first(c):
                pe.wait_ge(wo_in, 16 * 2)
                linear(wo, lambda k: qo[:, k, 0:MT], 2, out_evac, [c])

            def out_phase(l):
                for half in range(l, 2):
                    pe.wait_ge(wo_in, 16 * (l + 1))
                    pe.wait_ge(q_evac, CT * (2 * (l + 1) + (half if l == 0 else 0)))
                    if half and l == 1:
                        pe.wait_ge(out_evac, CT * 3)
                    linear(wo, lambda k: qo[:, k, half * MT:(half + 1) * MT], 2 * l + half, out_evac)
                    if l == 0:
                        q_half(1, half)

            def q_half(l, half):
                pe.wait_ge(wq_in, 16 * (l + 1))
                if l:
                    pe.wait_ge(out_evac, CT * (half + 1))
                else:
                    pe.wait_ge(xh_in, 16 * (half + 1))
                    if half:
                        pe.wait_ge(q_evac, CT)
                linear(wq, lambda k: xh[:, k, :], 2 * l + half, q_evac)

            def pairs(out, hi_lo_w, hi_lo_x, ks=range(KT), each_k=None):
                for k in ks:
                    if each_k:
                        each_k(k)
                    for m, (a, b) in enumerate(((0, 0), (0, 1), (1, 0))):
                        mm = nc.tensor.matmul(out, hi_lo_w[a](k), hi_lo_x[b](k), start=(k == 0 and m == 0),
                                              stop=(k == KT - 1 and m == 2))
                return mm

            def weights(w, g):
                return [lambda k, t=t: t[:, w, k, g * P:(g + 1) * P] for t in (w_hi, w_lo)]

            def tokens(a, b):
                return [lambda k, t=t: t[:, k, a:b] for t in (c_hi, c_lo)]

            def k_text(l, i):
                after(pe, row_free, row_use(l, i, "kt"))
                for g in range(G):
                    mm = pairs(rows[:, 0, g * TP:(g + 1) * TP], weights(0, g), tokens(0, TP))
                mm.then_inc(row_full, 1)

            def k_unit(l, i, g, c, ks=range(KT)):
                u = step(l, i, g)
                if ks[0] == 0:
                    after(pe, v_low, 2 * u - (0 if c or isinstance(i, int) and i < 0 else 1))
                each = (lambda k: pe.wait_ge(ctx_low[k % 2], i * (KT // 2) + (KT // 2 * (l * B + 1) + k // 2 + 1))) if g == G and c == 0 else None
                mm = pairs(banks[c][:, 0:HALF], weights(1, g % G), tokens(TP + c * HALF, TP + (c + 1) * HALF), ks, each)
                if ks[-1] == KT - 1:
                    mm.then_inc(k_full, 1)

            def v_unit(l, i, g, c, part):
                u = step(l, i, g)
                if part == 0:
                    pe.wait_ge(k_low, 2 * u + (c + 1))
                if c == 0:
                    if part == 0:
                        pairs(bankA[:, 0:TP], weights(2, g % G), tokens(0, TP))
                    mm = pairs(bankA[:, TP:TP + HALF], weights(3, g % G), tokens(TP, TP + HALF),
                               (range(0, 3), range(3, KT))[part])
                else:
                    mm = pairs(bankB[:, 0:HALF], weights(3, g % G), tokens(TP + HALF, TOKP),
                               (range(0, KT // 2), range(KT // 2, KT))[part])
                if part:
                    mm.then_inc(v_full, 1)

            def v_turn(l, i, g, c):
                u = step(l, i, g)
                pe.wait_ge(vT_ok, 2 * u + (c + 1))
                for n, t in enumerate(range(4) if c == 0 else range(4, NT)):
                    a = TP + (t - 1) * KEY if t else 0
                    mm = nc.tensor.transpose(banks[c][0:KEY, n * P:(n + 1) * P], vT[:, a:a + KEY], ident)
                mm.then_inc(vt_full, 1)

            def max_scores(l, i, g, h):
                t = step(l, i, g)
                if h == 0:
                    pe.wait_ge(q_high, t + 1)
                    pe.wait_ge(k_high, 2 * t + 2)
                    pe.wait_ge(kt_high, i + (l * B + 1))
                two = g == G - 1
                after(pe, row_free, row_use(l, i, f"max{h}", g) - (1 if two and h else 0))
                if two and h == 1:
                    after(pe, v_low, 2 * t + 2)
                out = proj if two and h % 2 else rows
                q = q_hi[:, g % 2, h, :]
                nc.tensor.matmul(out[0:S, 0, 0:HALF + TP], q, k_hi[:, g % 2, 0:HALF + TP], start=True, stop=True)
                nc.tensor.matmul(out[0:S, 1, 0:HALF], q, k_hi[:, g % 2, HALF + TP:TOKP],
                                 start=True, stop=True).then_inc(row_full, 1)

            def max_turn(l, i, g):
                after(pe, row_free, row_use(l, i, "shift", g))
                nc.tensor.transpose(rows[:, 0, 0:S], mx[:], ident[0:S, 0:S]).then_inc(row_full, 1)

            def context_turn(l, i):
                pe.wait_ge(ctx_chain, i * 6 + (6 * (l * B + 1) + 1))
                after(pe, row_free, row_use(l, i, "cmax", G - 3))
                nc.tensor.transpose(rows[:, 0, 0:P], cs[:, 0:1].to_broadcast([P, P]), ident).then_inc(row_full, 1)

            def score_tile(l, i, g, j):
                t = step(l, i, g)
                if j == 0:
                    after(pe, q_low, t + 1)
                    pe.wait_ge(k_low, 2 * t + 2)
                    pe.wait_ge(kt_low, i + (l * B + 1))
                if l and j > 2:
                    pe.wait_ge(sadd, (t - STEPS) * NIP + (j - 2))
                else:
                    after(pe, p_high, t * NT + max(j - 1, 0))
                n = KEY if j else TP
                out = st[0:n, j % 2, 0:Q4]
                a = (j - 1) * KEY + (TP if j > NIP // 2 else 0)
                hi = k_hi[:, g % 2, a:a + KEY] if j else kt_hi[:, g, :]
                lo = k_lo[:, g % 2, (j - 1) * KEY:j * KEY] if j else kt_lo[:, g, :]
                nc.tensor.matmul(out, hi, q_hi[:, g % 2], start=True, stop=False)
                nc.tensor.matmul(out, hi, q_lo[:, :, :], start=False, stop=False)
                nc.tensor.matmul(out, lo, q_hi[:, g % 2], start=False, stop=False)

            def add_shift(l, i, g, j):
                n = KEY if j else TP
                if j == 0:
                    after(pe, row_free, row_use(l, i, "shift", g) + 1)
                nc.tensor.matmul(st[0:n, j % 2, 0:Q4], sel[:, min(j, 1), 0:n], shift[:, :, :],
                                 start=False, stop=True).then_inc(s_full, 1)

            def weigh(l, i, g, half):
                t = step(l, i, g)
                if half == 0:
                    after(pe, p_low, t * NT + NT)
                    after(pe, v_low, 2 * t + 2)
                    after(pe, pv_read, t)
                for h in range(half * 2, half * 2 + 2):
                    for part, tiles in ((0, (0,)), (1, range(1, NT))):
                        for j in tiles:
                            n = TEXT if j == 0 else LAST if j == NT - 1 else KEY
                            for m, p in enumerate((p_hi, p_lo)):
                                mm = nc.tensor.matmul(pv[:, part, h * VS:(h + 1) * VS], p[0:n, j, h * S:h * S + P],
                                                      vst[0:n, g % 2, j, h, :], start=(j == tiles[0] and m == 0),
                                                      stop=(j == tiles[-1] and m == 1))
                if half:
                    mm.then_inc(pv_full, 1)

            def o_turn(l, i, g):
                pe.wait_ge(o_sum, step(l, i, g) + 1)
                after(pe, row_free, row_use(l, i, "oT", g))
                nc.tensor.transpose(rows[:, 0, 0:S], acc[:, 0].rearrange("s h d -> s (h d)"),
                                    ident[0:S, 0:S]).then_inc(row_full, 1)

            def project(l, i, g):
                return {
                    "K0": lambda: k_unit(l, i, g, 0), "K1": lambda: k_unit(l, i, g, 1),
                    "K1a": lambda: k_unit(l, i, g, 1, range(0, 3)),
                    "K1b": lambda: k_unit(l, i, g, 1, range(3, 5)), "K1c": lambda: k_unit(l, i, g, 1, range(5, KT)),
                    "V0a": lambda: v_unit(l, i, g, 0, 0), "V0b": lambda: v_unit(l, i, g, 0, 1),
                    "V1a": lambda: v_unit(l, i, g, 1, 0), "V1b": lambda: v_unit(l, i, g, 1, 1),
                    "T0": lambda: v_turn(l, i, g, 0), "T1": lambda: v_turn(l, i, g, 1),
                    "PVa": lambda: weigh(l, i, g - 2, 0), "PVb": lambda: weigh(l, i, g - 2, 1),
                }

            def semantic(l, i, unit):
                after(pe, qrow_ok, i + (l * B + 1))
                after(pe, row_free, row_use(l, i, "logit"))
                for g in range(G):
                    mm = nc.tensor.matmul(rows[0:S, 0, 0:TP], q_row[:, g, :], kt32[:, g, :],
                                          start=(g == 0), stop=(g == G - 1))
                mm.then_inc(row_full, 1)
                unit["K0"]()
                after(pe, row_free, row_use(l, i, "ti"))
                for c in range(2):
                    mm = pairs(rows[0:TP, c, 0:HALF], tokens(0, TP), tokens(TP + c * HALF, TP + (c + 1) * HALF))
                mm.then_inc(row_full, 1)
                unit["K1a"]()
                pe.wait_ge(probs, i * 5 + 5)
                after(pe, row_free, row_use(l, i, "pT"))
                nc.tensor.transpose(rows[:, 0, 0:S], mx[:], ident[0:S, 0:S]).then_inc(row_full, 1)
                unit["K1b"]()
                after(pe, row_free, row_use(l, i, "semq"))
                for c in range(2):
                    mm = nc.tensor.matmul(rows[0:S, c, 0:HALF], pT[:], ti[0:TEXT, c, :], start=True, stop=True)
                mm.then_inc(row_full, 1)
                unit["K1c"]()
                after(pe, row_free, row_use(l, i, "semk"))
                tif = ti[0:TEXT].rearrange("p c t -> p (c t)")
                for j in range(NIP):
                    mm = nc.tensor.matmul(rows[0:KEY, j // 3, j % 3 * S:(j % 3 + 1) * S],
                                          tif[:, j * KEY:(j + 1) * KEY], pT[:], start=True, stop=True)
                mm.then_inc(row_full, 1)

            FIRST = {0: ("K0", "K1", "V0a", "V0b", "V1a", "V1b", "", "T0", "T1", ""),
                     1: ("V0a", "V0b", "V1a", "V1b", "T0", "", "", "T1", "", "")}
            MIDDLE = ("K0", "K1", "PVa PVb", "V0a", "V0b", "V1a", "V1b", "T0", "T1", "")
            LAST_STEP = ("", "", "PVa", "", "PVb", "", "", "", "", "")

            def row(l, i):
                for g in range(G):
                    unit = project(l, i, g + 1)
                    places = [names.split() for names in
                              (FIRST[l] if g == 0 else LAST_STEP if g == G - 1 else MIDDLE)]

                    def fill(place):
                        for name in places[place]:
                            unit[name]()

                    if g == G - 1 and l and is_last(i):
                        for c in range(3):
                            unit[f"O{c}"] = lambda c=c: out_first(c)
                            places[7 + c] = [f"O{c}"]
                    if g == G - 1 and not is_last(i):
                        places[6], places[8] = ["K0"], ["K1"]
                    if l and g == 0:
                        semantic(l, i, unit)
                    for h in range(HG):
                        fill(h)
                        max_scores(l, i, g, h)
                    fill(4)
                    max_turn(l, i, g)
                    score_tile(l, i, g, 0), score_tile(l, i, g, 1)
                    add_shift(l, i, g, 0), add_shift(l, i, g, 1)
                    if 0 < g < G - 1:
                        o_turn(l, i, g - 1)
                    for j in range(2, NT):
                        if j == 4 and g == G - 3 and not (l and is_last(i)):
                            context_turn(l, i)
                        fill(3 + j)
                        score_tile(l, i, g, j)
                        add_shift(l, i, g, j)
                if is_last(i):
                    o_turn(l, i, G - 2)
                    if l:
                        out_first(3)
                    weigh(l, i, G - 1, 0), weigh(l, i, G - 1, 1)
                    if l:
                        out_first(4)
                    o_turn(l, i, G - 1)
                else:
                    k_text(l, i)
                    weigh(l, i, G - 1, 0)
                    o_turn(l, i, G - 2)
                    weigh(l, i, G - 1, 1)
                    for name in ("V0a", "V0b", "V1a", "T0", "V1b"):
                        unit[name]()
                    o_turn(l, i, G - 1)
                    unit["T1"]()

            pe.wait_ge(const_in, 64)
            for half in range(2):
                q_half(0, half)
            for l in range(LAYERS):
                pe.wait_ge(w_low, 16 * l + 4)
                pe.wait_ge(q_evac, 2 * CT * (l + 1))
                first = project(l, -1, G)
                first["K0"](), first["K1"]()
                pe.wait_ge(w_low, 16 * l + 8)
                k_text(l, -1)
                pe.wait_ge(w_low, 16 * l + 16)
                for name in ("V0a", "V0b", "V1a", "T0", "V1b", "T1"):
                    first[name]()
                pe.wait_ge(sel_ok, 2)
                pe.wait_ge(pads, l + 1)
                with pe.Fori(0, B - 1) as i:
                    row(l, i)
                row(l, B - 1)
                after(pe, row_free, row_use(l, B - 1, "oT", G - 1) + 1)
                out_phase(l)

        @block.scalar
        def _(act):
            loaded = set()

            def load_quarter(l, n):
                loaded.add((l, n))
                if before(l, n) is not None:
                    act.wait_ge(w_low, 16 * l + before(l, n) + 1)
                w, q = ORDER[n // 4], n % 4
                act.dma_start(slots[slot(l, n)], w_d[l * 4 + w][:, q * QW:(q + 1) * QW]).then_inc(w_in[slot(l, n)], 16)

            def split_weight(l, m, tiles=()):
                w, tiles = ORDER[m], iter(tiles)
                act.wait_ge(w_chain, 6 * (4 * l + m) + 6)
                for n in range(4 * m, 4 * m + 4):
                    a = n % 4 * QK
                    nc.scalar.activation(w_hi[:, w, a:a + QK, :].rearrange("p k c -> p (k c)"), slots[slot(l, n)],
                                         ACT.Copy, scale=wscale[:, w:w + 1]).then_inc(w_high, 1)
                    done = n if n % 4 == 3 else n - 1
                    for m2 in range(16):
                        if (l, m2) not in loaded and before(l, m2) is not None and before(l, m2) <= done:
                            load_quarter(l, m2)
                    place = next(tiles, None)
                    if place:
                        q_tiles(l, place[0], [place[1]])

            def split_context(n, k):
                if k % 2:
                    act.wait_ge(ctx_scaled, n * (KT // 2) + (k // 2 + 1))
                nc.scalar.activation(c_hi[:, k, :], ctx_raw[:, k, :], ACT.Copy,
                                     scale=1.0 if k % 2 else cs[:, 4:5]).then_inc(ctx_high, 1)

            def q_tiles(l, half, tiles):
                for c in tiles:
                    n = (CT * half + c) if l == 0 else 2 * CT + 2 * CT * half + CT + c
                    act.wait_ge(lin_full, n + 1)
                    nc.scalar.activation(qo[:, c, half * MT:(half + 1) * MT], banks[n % 2][:, 0:MT],
                                         ACT.Copy).then_inc(q_evac, 1)

            def k_text(l, i):
                act.wait_ge(row_full, row_use(l, i, "kt") + 1)
                after(act, s_full, i * G * NT + (l * STEPS + G) * NT)
                nc.scalar.activation(kt32[:].rearrange("p g t -> p (g t)"), rows[:, 0, 0:G * TP], ACT.Copy,
                                     scale=inv[:, 0:1]).then_inc(row_free, 1)
                after(act, row_free, row_use(l, i, "kt") + 1)
                nc.scalar.activation(kt_hi[:], kt32[:], ACT.Copy)
                nc.scalar.activation(k_hi[:, 0, HALF:HALF + TP], kt32[:, 0, :], ACT.Copy).then_inc(kt_high, 1)

            def k_unit(l, i, g, c):
                u = step(l, i, g)
                act.wait_ge(k_full, 2 * u + (c + 1))
                if g == G and c == 0:
                    act.wait_ge(inv_ok, i + (l * B + 2))
                after(act, s_full, (u if g == G else u - 1) * NT)
                if g < G and c == 0:
                    nc.scalar.activation(k_hi[:, g % 2, HALF:HALF + TP], kt32[:, g, :], ACT.Copy)
                a = c * (HALF + TP)
                nc.scalar.activation(k_hi[:, g % G % 2, a:a + HALF], banks[c][:, 0:HALF], ACT.Copy,
                                     scale=inv[:, 1:2]).then_inc(k_high, 1)

            def v_unit(l, i, g, c):
                u = step(l, i, g)
                act.wait_ge(v_full, 2 * u + (c + 1))
                after(act, vt_full, 2 * u)
                a, b = (0, TP + HALF) if c == 0 else (TP + HALF, TOKP)
                last = nc.scalar.activation(vT[:, a:b], banks[c][:, 0:b - a], ACT.Copy, scale=VSC)
                last.then_inc(vT_ok, 1)

            def v_turn(l, i, g, c):
                u = step(l, i, g)
                after(act, vt_full, 2 * u + (c + 1))
                after(act, pv_full, u if g == G else u - 1)
                a, b = (0, 4) if c == 0 else (4, NT)
                nc.scalar.activation(vst[0:KEY, g % G % 2, a:b, :, 0:D].rearrange("p t h d -> p (t h) d"),
                                     banks[c][0:KEY, 0:(b - a) * P].rearrange("p (n d) -> p n d", d=D),
                                     ACT.Copy).then_inc(v_high, 1)

            def q_high_part(l, i, g):
                t = step(l, i, g)
                act.wait_ge(qbd_ok, t + 1)
                after(act, s_full, (t if g == 0 else t - 1) * NT)
                nc.scalar.activation(q_hi[:, g % 2], qbd, ACT.Copy).then_inc(q_high, 1)

            def exps(l, i, g, j):
                t = step(l, i, g)
                if l and j:
                    act.wait_ge(sadd, (t - STEPS) * NIP + j)
                    src = prob[0:KEY, j % 3, :]
                else:
                    after(act, s_full, t * NT + (j + 1))
                    src = st[0:KEY if j else TP, j % 2, 0:Q4]
                if j == 0:
                    after(act, pv_full, t)
                after(act, p_low, t * NT + (j - 2 if j >= 3 else 0))
                n = KEY if j else TP
                nc.scalar.activation(p_hi[0:n, j, 0:Q4], src, ACT.Exp, scale=SC)
                nc.scalar.activation(prob[0:n, j % 3, :], src, ACT.Exp, scale=SC).then_inc(p_high, 1)

            def o_turn(l, i, g):
                act.wait_ge(row_full, row_use(l, i, "oT", g) + 1)
                nc.scalar.activation(qo[:, g, bass.ds(i * S, S)], rows[:, 0, 0:S], ACT.Copy).then_inc(row_free, 1)

            def project(l, i, g):
                return (lambda: k_unit(l, i, g, 0), lambda: k_unit(l, i, g, 1), lambda: v_unit(l, i, g, 0),
                        lambda: v_unit(l, i, g, 1), lambda: v_turn(l, i, g, 0), lambda: v_turn(l, i, g, 1))

            def nothing():
                return (lambda: None,) * 6

            def new_units(l, i):
                k0, k1, v0, v1, t0, t1 = project(l, i, G)
                k0(), k1()
                k_text(l, i)
                if not isinstance(i, int):
                    o_turn(l, i, G - 2)
                v0(), t0(), v1()
                if not isinstance(i, int):
                    o_turn(l, i, G - 1)
                t1()

            def row(l, i):
                if l:
                    act.wait_ge(row_full, row_use(l, i, "logit") + 1)
                    act.wait_ge(probs, i * 5 + 2)
                    nc.scalar.activation(mx[:, 0:TEXT], rows[0:S, 0, 0:TEXT], ACT.Exp, bias=sm[:, 1:2],
                                         scale=SC).then_inc(row_free, 1)
                for g in range(G):
                    k0, k1, v0, v1, t0, t1 = project(l, i, g + 1) if g < G - 1 else nothing()
                    if g == 0:
                        q_high_part(l, i, g)
                    k0()
                    new_context = g >= G - 2 and not (l and is_last(i))
                    if new_context and g == G - 1:
                        for k in range(EARLY, KT):
                            split_context(i + (l * B + 1), k)
                    k1()
                    v0()
                    exps(l, i, g, 0)
                    if 0 < g < G - 1:
                        o_turn(l, i, g - 1)
                    exps(l, i, g, 1)
                    exps(l, i, g, 2)
                    v1()
                    if g < G - 1:
                        q_high_part(l, i, g + 1)
                    if new_context and g == G - 2:
                        act.wait_ge(ctx_chain, i * 6 + 6 * (l * B + 2))
                    exps(l, i, g, 3)
                    t0()
                    if new_context and g == G - 2:
                        split_context(i + (l * B + 1), 0)
                    exps(l, i, g, 4)
                    t1()
                    exps(l, i, g, 5)
                    if new_context and g == G - 2:
                        split_context(i + (l * B + 1), 1)
                    exps(l, i, g, 6)
                if is_last(i):
                    o_turn(l, i, G - 2)
                    o_turn(l, i, G - 1)
                else:
                    new_units(l, i)

            for n in range(4):
                load_quarter(0, n)
            split_weight(0, 0)
            q_tiles(0, 0, range(1))
            act.wait_ge(ctx_chain, 6)
            for k in range(KT):
                split_context(0, k)
            q_tiles(0, 0, [1, 2])
            split_contexts(act, 1)
            load_quarter(0, 8), load_quarter(0, 9)
            q_tiles(0, 0, [3])
            split_weight(0, 1, [(0, 4)])
            q_tiles(0, 1, [0, 1])
            split_weight(0, 2, [None, (1, 2)])
            q_tiles(0, 1, [3, 4])
            split_weight(0, 3)
            for l in range(LAYERS):
                new_units(l, -1)
                with act.Fori(0, B - 1) as i:
                    row(l, i)
                row(l, B - 1)
                if l == 0:
                    split_contexts(act, B + 1)
                    after(act, pv_full, STEPS)
                    for n in range(SLOTS):
                        load_quarter(1, n)
                    split_weight(1, 0)
                    q_tiles(1, 0, range(1))
                    split_weight(1, 1, [None, (0, 1)])
                    q_tiles(1, 0, range(2, CT))
                    split_weight(1, 2)
                    split_weight(1, 3)
                    q_tiles(1, 1, range(CT))

        @block.gpsimd
        def _(pool):
            def all_max(ap, chain, n):
                pool.wait_ge(chain, n)
                nc.gpsimd.partition_all_reduce(ap[:, 1:2], ap[:, 0:1], P, RMAX).then_inc(chain, 1)

            def ones_and_pads(l):
                for b in range(2):
                    nc.gpsimd.memset(vst[:, b, :, :, 2 * D:VS].rearrange("p t h v -> p (t h) v"), 1.0)
                for p in (p_hi, p_lo):
                    last = nc.gpsimd.memset(p[:, :, Q4:PW], 0.0)
                last.then_inc(pads, 1)

            def q_spread(l, i, g):
                t = step(l, i, g)
                after(pool, q_low, t)
                if g == G:
                    if l and not isinstance(i, int):
                        pool.wait_ge(row_full, row_use(l, i, "logit") + 1)
                    nc.gpsimd.tensor_copy(q_row, qo[:, :, bass.ds(i * S + S, S)]).then_inc(qrow_ok, 1)
                    after(pool, qrow_ok, i + (l * B + 2))
                nc.gpsimd.tensor_tensor(qbd, q_row[:, g % G, :].unsqueeze(1).to_broadcast([P, HG, S]),
                                        hmask.unsqueeze(2).to_broadcast([P, HG, S]), ALU.mult).then_inc(qbd_ok, 1)

            def scale_context(n, k):
                if k == 1:
                    pool.wait_ge(ctx_chain, n * 6 + 6)
                nc.gpsimd.tensor_tensor(ctx_raw[:, k, :], ctx_raw[:, k, :], cs[:, 4:5].to_broadcast([P, TOKP]),
                                        ALU.mult).then_inc(ctx_scaled, 1)

            def split_context(n, k):
                pool.wait_ge(ctx_high, n * KT + (k + 1))
                nc.gpsimd.tensor_tensor(c_lo[:, k, :], ctx_raw[:, k, :], c_hi[:, k, :],
                                        ALU.subtract).then_inc(ctx_low[1], 1)

            def row(l, i):
                for g in range(1, G - 1):
                    q_spread(l, i, g)
                if not (l and is_last(i)):
                    for k in range(1, KT, 2):
                        scale_context(i + (l * B + 1), k)
                q_spread(l, i, G - 1)
                if not (l and is_last(i)):
                    for k in range(1, KT, 2):
                        split_context(i + (l * B + 1), k)
                if not is_last(i):
                    q_spread(l, i, G)

            for n, s in enumerate(PRIMED):
                nc.gpsimd.memset(primer[:, n:n + 1], 0.0).then_inc(s, 1)
            for l in range(LAYERS):
                for m in range(4):
                    all_max(ws, w_chain, 6 * (4 * l + m) + 1)
                    if l == 0 and m == 0:
                        all_max(cs, ctx_chain, 1)
                        for k in range(1, KT, 2):
                            scale_context(0, k)
                        for k in range(1, KT, 2):
                            split_context(0, k)
                pool.wait_ge(w_low, 16 * (l + 1))
                pool.wait_ge(q_evac, 2 * CT * (l + 1))
                if l:
                    pool.wait_ge(out_evac, 2 * CT)
                    pool.wait_ge(x1_out, 32)
                ones_and_pads(l)
                q_spread(l, -1, G)
                with pool.Fori(0, B - 1) as i:
                    row(l, i)
                row(l, B - 1)

        @block.vector
        def _(dve):
            def scale_chain(ap, chain, base, s_out, inv_out):
                dve.wait_ge(chain, base + 2)
                nc.vector.tensor_scalar(ap[:, 2:3], ap[:, 1:2], TINY, None, ALU.max).then_inc(chain, 1)
                dve.wait_ge(chain, base + 3)
                nc.vector.tensor_scalar(ap[:, 3:4].bitcast(I32), ap[:, 2:3].bitcast(I32), EXP_BITS, None,
                                        ALU.bitwise_and).then_inc(chain, 1)
                dve.wait_ge(chain, base + 4)
                nc.vector.tensor_scalar(inv_out, ap[:, 3:4], 1.0 / TOP, None, ALU.mult).then_inc(chain, 1)
                dve.wait_ge(chain, base + 5)
                nc.vector.reciprocal(s_out, inv_out).then_inc(chain, 1)

            def weight_part(l, n):
                dve.wait_ge(w_in[slot(l, n)], arrived(l, n))
                nc.vector.tensor_reduce(wparts[:, n // 4 % 2, n % 4:n % 4 + 1], slots[slot(l, n)], AX.X, ALU.max,
                                        apply_absolute_value=True).then_inc(w_parts, 1)

            def weight_scale(l, m):
                w = ORDER[m]
                dve.wait_ge(w_parts, 16 * l + 4 * m + 4)
                nc.vector.tensor_reduce(ws[:, 0:1], wparts[:, m % 2], AX.X, ALU.max).then_inc(w_chain, 1)
                scale_chain(ws, w_chain, 6 * (4 * l + m), wscale[:, w:w + 1], winv[:, w:w + 1])

            def weight_low(l, n):
                w, a = ORDER[n // 4], n % 4 * QK
                dve.wait_ge(w_high, 16 * l + n + 1)
                nc.vector.scalar_tensor_tensor(w_lo[:, w, a:a + QK, :].rearrange("p k c -> p (k c)"), slots[slot(l, n)],
                                               wscale[:, w:w + 1], w_hi[:, w, a:a + QK, :].rearrange("p k c -> p (k c)"),
                                               ALU.mult, ALU.subtract).then_inc(w_low, 1)

            def weight(l, m, tiles=()):
                tiles = iter(tiles)

                def tile():
                    place = next(tiles, None)
                    if place:
                        out_tile(0, *place)

                weight_part(l, 4 * m), weight_part(l, 4 * m + 1)
                tile()
                weight_part(l, 4 * m + 2)
                tile()
                weight_part(l, 4 * m + 3)
                weight_scale(l, m)
                tile()
                weight_low(l, 4 * m), weight_low(l, 4 * m + 1)
                tile()
                weight_low(l, 4 * m + 2), weight_low(l, 4 * m + 3)
                tile()

            def context_part(n, k):
                if k == 0:
                    dve.wait_ge(ctx_in, n * 16 + 16)
                nc.vector.tensor_reduce(cparts[:, k:k + 1], ctx_raw[:, k, :], AX.X, ALU.max,
                                        apply_absolute_value=True).then_inc(ctx_parts, 1)

            def context_max(n):
                dve.wait_ge(ctx_parts, n * KT + KT)
                nc.vector.tensor_reduce(cs[:, 0:1], cparts[:], AX.X, ALU.max).then_inc(ctx_chain, 1)

            def context_turn(l, i):
                dve.wait_ge(row_full, row_use(l, i, "cmax", G - 3) + 1)
                nc.vector.tensor_reduce(cs[:, 1:2], rows[:, 0, 0:P], AX.X, ALU.max).then_inc(ctx_chain, 1)
                dve.wait_ge(ctx_chain, i * 6 + (6 * (l * B + 1) + 2))
                nc.vector.tensor_copy(cs[:, 6:7], cs[:, 1:2]).then_inc(row_free, 1)

            def context_scale(n):
                scale_chain(cs, ctx_chain, n * 6, cs[:, 4:5], cs[:, 5:6])

            def split_context(n, k):
                dve.wait_ge(ctx_high, n * KT + (k + 1))
                nc.vector.scalar_tensor_tensor(c_lo[:, k, :], ctx_raw[:, k, :], cs[:, 4:5], c_hi[:, k, :],
                                               ALU.mult, ALU.subtract).then_inc(ctx_low[0], 1)

            def out_tile(l, half, c):
                dve.wait_ge(xh_in, 16 * (2 * (l + 1) + half + 1))
                n = 2 * CT + (2 * CT * half if l == 0 else 4 * CT + CT * half) + c
                dve.wait_ge(lin_full, n + 1)
                x = xr if l and half == 0 else xh
                nc.vector.scalar_tensor_tensor(x[:, c, :], banks[n % 2][:, 0:MT], bias[:, l, c:c + 1], x[:, c, :],
                                               ALU.add, ALU.add).then_inc(out_evac, 1)

            def k_text(l, i):
                dve.wait_ge(kt_high, i + (l * B + 2))
                nc.vector.tensor_tensor(kt_lo[:], kt32[:], kt_hi[:].bitcast(F32), ALU.subtract).then_inc(kt_low, 1)

            def k_unit(l, i, g, c):
                u = step(l, i, g)
                dve.wait_ge(k_high, 2 * u + (c + 1))
                a, b = c * HALF, (c + 1) * HALF
                a2 = c * (HALF + TP)
                nc.vector.scalar_tensor_tensor(k_lo[:, g % G % 2, a:b], banks[c][:, 0:HALF], inv[:, 1:2],
                                               k_hi[:, g % G % 2, a2:a2 + HALF].bitcast(F32), ALU.mult, ALU.subtract).then_inc(k_low, 1)

            def v_turn(l, i, g, c):
                u = step(l, i, g)
                dve.wait_ge(v_high, 2 * u + (c + 1))
                a, b = (0, 4) if c == 0 else (4, NT)
                high, low = (vst[0:KEY, g % G % 2, a:b, :, m * D:(m + 1) * D].rearrange("p t h d -> p (t h) d")
                             for m in range(2))
                nc.vector.tensor_tensor(low, banks[c][0:KEY, 0:(b - a) * P].rearrange("p (n d) -> p n d", d=D), high,
                                        ALU.subtract).then_inc(v_low, 1)

            def q_low_part(l, i, g):
                dve.wait_ge(q_high, step(l, i, g) + 1)
                after(dve, s_full, step(l, i, g) * NT)
                nc.vector.tensor_tensor(q_lo[:], qbd, q_hi[:, g % 2].bitcast(F32), ALU.subtract).then_inc(q_low, 1)

            def maxima(l, i, g, h):
                dve.wait_ge(row_full, row_use(l, i, f"max{h}", g) + 1)
                if l and h and g == G - 1:
                    after(dve, row_free, row_use(l, i, f"max{h}", g))
                src = proj if g == G - 1 and h % 2 else rows
                nc.vector.tensor_reduce(mx[:, h:h + 1], src[0:S, 0, HALF:HALF + TP], AX.X, ALU.max)
                if l:
                    last = nc.vector.tensor_tensor_reduce(out=ti[0:S], in0=src[0:S, :, 0:HALF], in1=semq, scale=1.0,
                                                          scalar=LOWEST, op0=ALU.add, op1=ALU.max,
                                                          accum_out=mx[:, HG + h:HG + h + 1])
                else:
                    last = nc.vector.tensor_reduce(mx[:, HG + h:HG + h + 1], src[0:S, :, 0:HALF], AX.XY, ALU.max)
                last.then_inc(row_free, 1)

            def shift_build(l, i, g):
                dve.wait_ge(row_full, row_use(l, i, "shift", g) + 1)
                after(dve, s_full, step(l, i, g) * NT)
                nc.vector.tensor_tensor(shift[:], rows[:, 0, 0:S].unsqueeze(1).to_broadcast([P, HG, S]),
                                        nmask.unsqueeze(2).to_broadcast([P, HG, S]), ALU.mult).then_inc(row_free, 1)

            def add_semantic(l, i, g, j):
                t = step(l, i, g)
                after(dve, s_full, t * NT + (j + 1))
                after(dve, p_low, t * NT + (j - 2 if j >= 3 else 0))
                nc.vector.tensor_tensor(prob[0:KEY, j % 3, :].rearrange("p (h q) -> p h q", h=HG),
                                        st[0:KEY, j % 2, 0:Q4].rearrange("p (h q) -> p h q", h=HG),
                                        semk[:, j - 1, :].unsqueeze(1).to_broadcast([KEY, HG, S]),
                                        ALU.add).then_inc(sadd, 1)

            def prob_low(l, i, g, j):
                t = step(l, i, g)
                after(dve, p_high, t * NT + (j + 1))
                n = KEY if j else TP
                nc.vector.tensor_tensor(p_lo[0:n, j, 0:Q4], prob[0:n, j % 3, :], p_hi[0:n, j, 0:Q4],
                                        ALU.subtract).then_inc(p_low, 1)

            def normalise(l, i, g):
                t = step(l, i, g)
                after(dve, pv_full, t + 1)
                out = pv[0:S, :, 0:HG * VS].rearrange("s b (h v) -> s b h v", h=HG)
                nc.vector.reciprocal(den[:], out[:, :, :, 2 * D]).then_inc(norm, 1)
                for b in range(2):
                    nc.vector.tensor_reduce(acc[:, b], out[:, b, :, 0:2 * D].rearrange("s h (m d) -> s h d m", m=2),
                                            AX.X, ALU.add).then_inc(pv_read if b else norm, 1)
                dve.wait_ge(back_ok, i * 2 + 2 * (l * B + 1))
                dve.wait_ge(norm, t * 4 + 1)
                nc.vector.tensor_tensor(den[:], den[:], back[:].unsqueeze(2).to_broadcast([S, 2, HG]),
                                        ALU.mult).then_inc(norm, 1)
                dve.wait_ge(norm, t * 4 + 3)
                after(dve, pv_read, t + 1)
                nc.vector.tensor_tensor(acc, acc, den[:].unsqueeze(3).to_broadcast([S, 2, HG, D]),
                                        ALU.mult).then_inc(norm, 1)
                dve.wait_ge(norm, t * 4 + 4)
                nc.vector.tensor_tensor(acc[:, 0], acc[:, 0], acc[:, 1], ALU.add).then_inc(o_sum, 1)

            def scale_back(l, i):
                if l or not isinstance(i, int):
                    dve.wait_ge(o_sum, step(l, i, G))
                for b in range(2):
                    nc.vector.tensor_scalar(back[:, b:b + 1], inv[0:S, 2 + b:3 + b], 1.0 / VSC,
                                            mask[:, l:l + 1] if b else None, ALU.mult,
                                            *([ALU.mult] if b else [])).then_inc(back_ok, 1)

            def project(l, i, g):
                return (lambda: k_unit(l, i, g, 0), lambda: k_unit(l, i, g, 1), lambda: v_turn(l, i, g, 0),
                        lambda: v_turn(l, i, g, 1))

            OUT_TILES = {(1, 0): [(0, c) for c in range(CT)],
                         (1, 2): [None, None, None, (1, 0), (1, 1)],
                         (1, 3): [(1, 2), (1, 3), (1, 4)]}

            def new_scale(l, i):
                if l or not isinstance(i, int):
                    dve.wait_ge(vT_ok, 2 * step(l, i, G))
                dve.wait_ge(ctx_chain, i * 6 + 6 * (l * B + 2))
                nc.vector.tensor_scalar(inv[:], winv[:], cs[:, 5:6], None, ALU.mult).then_inc(inv_ok, 1)

            def new_units(l, i):
                k0, k1, t0, t1 = project(l, i, G)
                k0(), k1()
                k_text(l, i)
                if not isinstance(i, int):
                    normalise(l, i, G - 1)
                t0()
                dve.wait_ge(inv_ok, i + (l * B + 2))
                scale_back(l, i)
                t1()

            def semantic(l, i, k0, k1):
                dve.wait_ge(row_full, row_use(l, i, "logit") + 1)
                nc.vector.tensor_reduce(sm[:, 0:1], rows[0:S, 0, 0:TEXT], AX.X, ALU.max).then_inc(probs, 1)
                dve.wait_ge(probs, i * 5 + 1)
                nc.vector.tensor_scalar(sm[:, 1:2], sm[:, 0:1], -SC, None, ALU.mult).then_inc(probs, 1)
                q_low_part(l, i, 0)
                after(dve, row_free, row_use(l, i, "logit") + 1)
                nc.vector.tensor_reduce(sm[:, 2:3], mx[:, 0:TEXT], AX.X, ALU.add).then_inc(probs, 1)
                dve.wait_ge(probs, i * 5 + 3)
                nc.vector.reciprocal(sm[:, 3:4], sm[:, 2:3]).then_inc(probs, 1)
                dve.wait_ge(probs, i * 5 + 4)
                nc.vector.tensor_scalar(mx[:, 0:TEXT], mx[:, 0:TEXT], sm[:, 3:4], None, ALU.mult).then_inc(probs, 1)
                k0()
                dve.wait_ge(row_full, row_use(l, i, "ti") + 1)
                nc.vector.tensor_scalar(ti[0:TP], rows[0:TP, :, 0:HALF], cs[0:TP, 5:6], cs[0:TP, 5:6],
                                        ALU.mult, ALU.mult).then_inc(row_free, 1)
                dve.wait_ge(row_full, row_use(l, i, "pT") + 1)
                nc.vector.tensor_copy(pT[:], rows[0:TEXT, 0, 0:S]).then_inc(row_free, 1)
                dve.wait_ge(row_full, row_use(l, i, "semq") + 1)
                nc.vector.tensor_scalar(semq, rows[0:S, :, 0:HALF], SEM, None, ALU.mult).then_inc(row_free, 1)
                dve.wait_ge(row_full, row_use(l, i, "semk") + 1)
                nc.vector.tensor_scalar(semk.rearrange("p (b t) q -> p b (t q)", b=2),
                                        rows[0:KEY, :, 0:NIP // 2 * S], SEM, None, ALU.mult).then_inc(row_free, 1)
                k1()

            def row(l, i):
                for g in range(G):
                    k0, k1, t0, t1 = project(l, i, g + 1) if g < G - 1 else (lambda: None,) * 4
                    new_context = not (l and is_last(i))
                    splits = iter(range(0, KT, 2)) if g == G - 1 and new_context else iter(())

                    def split(count):
                        for _, k in zip(range(count), splits):
                            split_context(i + (l * B + 1), k)

                    if l and g == 0:
                        semantic(l, i, k0, k1)
                    else:
                        q_low_part(l, i, g)
                        k0()
                    if g == G - 1 and not is_last(i):
                        new_scale(l, i)
                    maxima(l, i, g, 0)
                    maxima(l, i, g, 1)
                    if not (l and g == 0):
                        k1()
                    maxima(l, i, g, 2)
                    if 0 < g < G - 1:
                        normalise(l, i, g - 1)
                    maxima(l, i, g, 3)
                    shift_build(l, i, g)
                    split(2)
                    for j in range(NT):
                        if g == G - 1 and j == 3:
                            normalise(l, i, g - 1)
                        if l and j < NT - 1:
                            add_semantic(l, i, g, j + 1)
                        prob_low(l, i, g, j)
                        if g == G - 3 and j == 0 and new_context:
                            context_max(i + (l * B + 1))
                        if g == G - 3 and j == 3 and new_context:
                            context_turn(l, i)
                            context_scale(i + (l * B + 1))
                        if l and is_last(i) and g == G - 1 and j >= 3:
                            out_tile(1, 0, j - 3)
                        if j == 3:
                            t0()
                        if j == 4:
                            t1()
                        if j < 2:
                            split(1)
                        if g < 2 and j in (1, 3, 5, 6) and new_context:
                            context_part(i + (l * B + 1), 4 * g + (1, 3, 5, 6).index(j))
                if is_last(i):
                    normalise(l, i, G - 1)
                    if l:
                        out_tile(1, 0, CT - 1)
                else:
                    new_units(l, i)

            dve.wait_ge(const_in, 64)
            nc.vector.tensor_copy(sel[:].rearrange("p a k -> p (a k)"), sel_raw).then_inc(sel_ok, 1)
            nc.vector.memset(mx[:], 0.0).then_inc(sel_ok, 1)
            for n in range(4):
                weight_part(0, n)
            weight_scale(0, 0)
            for n in range(4):
                weight_low(0, n)
            for k in range(KT):
                context_part(0, k)
            context_max(0)
            context_scale(0)
            for k in range(0, KT, 2):
                split_context(0, k)
            for l in range(LAYERS):
                for m in range(1 - l, 4):
                    weight(l, m, OUT_TILES.get((l, m), ()))
                dve.wait_ge(w_chain, 24 * (l + 1))
                if l:
                    split_contexts(dve, B + 1)
                    dve.wait_ge(x1_out, 32)
                new_scale(l, -1)
                new_units(l, -1)
                with dve.Fori(0, B - 1) as i:
                    row(l, i)
                row(l, B - 1)
            for c in range(CT):
                out_tile(1, 1, c)


def kernel(x, ctx_2048, fside_S_0, L0_xattn_Wq, L0_xattn_Wk, L0_xattn_Wv, L0_xattn_Wk_ip, L0_xattn_Wv_ip,
           L0_xattn_Wo, L0_xattn_bo, L1_xattn_Wq, L1_xattn_Wk, L1_xattn_Wv, L1_xattn_Wk_ip, L1_xattn_Wv_ip,
           L1_xattn_Wout, L1_xattn_bout):
    import concourse.bacc as bacc
    from concourse.bass_utils import run_bass_kernel_spmd

    def rows_first(w):
        w = np.asarray(w)
        return w.reshape(-1, P, w.shape[1]).transpose(1, 0, 2).reshape(P, -1)

    ctx = np.asarray(ctx_2048)
    order = list(range(TEXT)) + [TEXT - 1] + list(range(TEXT, TOK)) + [TOK - 1] * (IPP - IP)
    ctx = ctx[:, order, :].transpose(0, 2, 1).reshape(B, KT, P, TOKP).transpose(0, 2, 1, 3).reshape(B, P, KT * TOKP)
    ctx = np.concatenate([ctx, ctx[:1]])
    xs = np.asarray(x).reshape(2, MT, CT, P).transpose(0, 3, 2, 1)
    weights = [np.asarray(w).T for w in (L0_xattn_Wk, L0_xattn_Wk_ip, L0_xattn_Wv, L0_xattn_Wv_ip)]
    weights += [np.asarray(w) for w in (L1_xattn_Wk, L1_xattn_Wk_ip, L1_xattn_Wv, L1_xattn_Wv_ip)]
    const = np.zeros((P, P + 2 * HG + 2 * KEY), np.float32)
    const[:, 0:P] = np.eye(P)
    const[0:HG, P + 2 * HG:P + 2 * HG + KEY] = 1.0
    const[HG:2 * HG, P + 2 * HG + KEY:] = 1.0
    for h in range(HG):
        const[h * D:(h + 1) * D, P + h] = 1.0
        const[[h, HG + h], P + HG + h] = -1.0
    arrays = {
        "ctx": ctx,
        "x": xs,
        "w": np.stack([rows_first(w) for w in weights]),
        "wq": np.stack([rows_first(np.asarray(L0_xattn_Wq).T), rows_first(L1_xattn_Wq)]).reshape(LAYERS, P, CT, C),
        "wo": np.stack([rows_first(np.asarray(L0_xattn_Wo).T), rows_first(L1_xattn_Wout)]).reshape(LAYERS, P, CT, C),
        "bias": np.stack([np.asarray(b).reshape(CT, P).T for b in (L0_xattn_bo, L1_xattn_bout)], axis=1),
        "mask": np.stack([np.ones(S, np.float32), np.asarray(fside_S_0)], axis=1),
        "const": const,
    }
    arrays = {f"{n}_dram": np.ascontiguousarray(a) for n, a in arrays.items()}
    nc = bacc.Bacc("TRN2", target_bir_lowering=False, num_devices=1)
    ins = [nc.dram_tensor(n, a.shape, mybir.dt.from_np(a.dtype), kind="ExternalInput").ap() for n, a in arrays.items()]
    x1 = nc.dram_tensor("x1_dram", (2, P, CT, MT), F32, kind="Internal").ap()
    out = nc.dram_tensor("out_dram", (2, P, CT, MT), F32, kind="ExternalOutput").ap()
    xattn_pair_kernel(nc, *ins, x1, out)
    got = run_bass_kernel_spmd(nc, [arrays], core_ids=[0]).results[0]["out_dram"]
    return got.transpose(0, 3, 2, 1).reshape(B, S, C)
```
